# Optimizing a Trainium2 kernel written in Bass

```python
import numpy as np
import jax
import jax.numpy as jnp

def _softmax(x, axis=-1):
    return jax.nn.softmax(x, axis=axis)

def _gelu(x):
    return jax.nn.gelu(x, approximate=True)

def _silu(x):
    return jax.nn.silu(x)

def _sigmoid(x):
    return jax.nn.sigmoid(x)

def _layernorm(x, axis=-1, eps=1e-05):
    m = jnp.mean(x, axis=axis, keepdims=True)
    v = jnp.var(x, axis=axis, keepdims=True)
    return (x - m) / jnp.sqrt(v + eps)

def _scatter_add(tgt, idx, src, axis=0):
    return tgt.at[idx].add(src)

def _segment_sum(src, seg, n):
    return jax.ops.segment_sum(src, seg, n)
kernel_name = 'mk_recurrent_d1_jaxref_r8_47ee75'

def setup_inputs(seed: int=0):
    np.random.seed(seed)
    _w = jnp.asarray

    def _L0_attn_setup():
        import jax, jax.numpy as jnp
        import numpy as np
        EPS = 1e-05
        CHUNK = 128

        def lightning_attn(q, k, v, ld, chunk=CHUNK):
            b, n, h, d = q.shape
            nc = n // chunk
            idx = jnp.arange(chunk)
            diff = idx[:, None] - idx[None, :]
            mask = diff >= 0
            D = jnp.exp(ld[:, None, None] * jnp.where(mask, diff, 0)) * mask
            q_decay = jnp.exp(ld[None, :] * (idx + 1)[:, None])
            k_decay = jnp.exp(ld[None, :] * (chunk - 1 - idx)[:, None])
            chunk_decay = jnp.exp(ld * chunk)
            qc = jnp.moveaxis(q.reshape(b, nc, chunk, h, d), 1, 0)
            kc = jnp.moveaxis(k.reshape(b, nc, chunk, h, d), 1, 0)
            vc = jnp.moveaxis(v.reshape(b, nc, chunk, h, d), 1, 0)

            def step(S, inp):
                qb, kb, vb = inp
                scores = jnp.einsum('bchd,bshd->bhcs', qb, kb) * D[None]
                o_intra = jnp.einsum('bhcs,bshd->bchd', scores, vb)
                o_inter = jnp.einsum('bchd,bhde->bche', qb, S) * q_decay[None, :, :, None]
                S_new = chunk_decay[None, :, None, None] * S + jnp.einsum('bshd,bshe->bhde', kb * k_decay[None, :, :, None], vb)
                return (S_new, o_intra + o_inter)
            S0 = jnp.zeros((b, h, d, d), dtype=q.dtype)
            S_final, oc = jax.lax.scan(step, S0, (qc, kc, vc))
            out = jnp.moveaxis(oc, 0, 1).reshape(b, n, h, d)
            return (out, S_final)

        def group_rmsnorm_fused_gate(o, gate, w, num_heads):
            b, n, d = o.shape
            hd = d // num_heads
            o = o * jax.nn.sigmoid(gate)
            og = o.reshape(b, n, num_heads, hd)
            og = og * jax.lax.rsqrt(jnp.mean(og * og, axis=-1, keepdims=True) + EPS)
            return og.reshape(b, n, d) * w
        key = jax.random.key(seed)
        ks = jax.random.split(key, 10)
        B, N, D, H = (2, 512, 256, 16)
        HD = D // H
        s = 1.0 / np.sqrt(D)
        x = jax.random.normal(ks[0], (B, N, D), dtype=jnp.float32)
        log_decay = -jax.random.uniform(ks[1], (H,), dtype=jnp.float32, minval=0.01, maxval=1.0)
        Wq = jax.random.normal(ks[2], (D, D), dtype=jnp.float32) * s
        Wk = jax.random.normal(ks[3], (D, D), dtype=jnp.float32) * s
        Wv = jax.random.normal(ks[4], (D, D), dtype=jnp.float32) * s
        Wo = jax.random.normal(ks[5], (D, D), dtype=jnp.float32) * s
        Wg1 = jax.random.normal(ks[6], (D, HD), dtype=jnp.float32) * s
        Wg2 = jax.random.normal(ks[7], (HD, D), dtype=jnp.float32) / np.sqrt(HD)
        norm_w = jnp.ones((D,), dtype=jnp.float32)
        return {'x': x, 'log_decay': log_decay, 'Wq': Wq, 'Wk': Wk, 'Wv': Wv, 'Wo': Wo, 'Wg1': Wg1, 'Wg2': Wg2, 'norm_w': norm_w}
    _L0_attn_in = _L0_attn_setup()

    def _L0_ffn_setup():
        import jax, jax.numpy as jnp
        import numpy as np
        FP8 = jnp.float8_e4m3fn
        key = jax.random.key(seed)
        k1, k2 = jax.random.split(key)
        input1 = jax.random.normal(k1, (2, 512, 256), dtype=jnp.float32)
        input2 = jax.random.normal(k2, (256, 256), dtype=jnp.float32)
        scale = jnp.array(0.5, dtype=jnp.float32)
        scale1 = jnp.array(0.5, dtype=jnp.float32)
        return {'input1': input1, 'input2': input2, 'scale': scale, 'scale1': scale1}
    _L0_ffn_in = _L0_ffn_setup()
    _d = {'L0_attn_x': _L0_attn_in['x'], 'L0_attn_log_decay': _L0_attn_in['log_decay'], 'L0_attn_Wq': _L0_attn_in['Wq'], 'L0_attn_Wk': _L0_attn_in['Wk'], 'L0_attn_Wv': _L0_attn_in['Wv'], 'L0_attn_Wo': _L0_attn_in['Wo'], 'L0_attn_Wg1': _L0_attn_in['Wg1'], 'L0_attn_Wg2': _L0_attn_in['Wg2'], 'L0_attn_norm_w': _L0_attn_in['norm_w'], 'L0_ffn_input2': _L0_ffn_in['input2'], 'L0_ffn_scale': _L0_ffn_in['scale'], 'L0_ffn_scale1': _L0_ffn_in['scale1']}
    _x0 = _d['L0_attn_x']
    _d['L0_attn_x'] = jax.random.normal(jax.random.fold_in(jax.random.key(seed), 1), (4, 512, 256), dtype=_x0.dtype)
    del _x0
    return _d

def reference(L0_attn_x, L0_attn_log_decay, L0_attn_Wq, L0_attn_Wk, L0_attn_Wv, L0_attn_Wo, L0_attn_Wg1, L0_attn_Wg2, L0_attn_norm_w, L0_ffn_input2, L0_ffn_scale, L0_ffn_scale1):

    def _L0_attn_ref(x, log_decay, Wq, Wk, Wv, Wo, Wg1, Wg2, norm_w):
        import jax, jax.numpy as jnp
        import numpy as np
        EPS = 1e-05
        CHUNK = 128

        def lightning_attn(q, k, v, ld, chunk=CHUNK):
            b, n, h, d = q.shape
            nc = n // chunk
            idx = jnp.arange(chunk)
            diff = idx[:, None] - idx[None, :]
            mask = diff >= 0
            D = jnp.exp(ld[:, None, None] * jnp.where(mask, diff, 0)) * mask
            q_decay = jnp.exp(ld[None, :] * (idx + 1)[:, None])
            k_decay = jnp.exp(ld[None, :] * (chunk - 1 - idx)[:, None])
            chunk_decay = jnp.exp(ld * chunk)
            qc = jnp.moveaxis(q.reshape(b, nc, chunk, h, d), 1, 0)
            kc = jnp.moveaxis(k.reshape(b, nc, chunk, h, d), 1, 0)
            vc = jnp.moveaxis(v.reshape(b, nc, chunk, h, d), 1, 0)

            def step(S, inp):
                qb, kb, vb = inp
                scores = jnp.einsum('bchd,bshd->bhcs', qb, kb) * D[None]
                o_intra = jnp.einsum('bhcs,bshd->bchd', scores, vb)
                o_inter = jnp.einsum('bchd,bhde->bche', qb, S) * q_decay[None, :, :, None]
                S_new = chunk_decay[None, :, None, None] * S + jnp.einsum('bshd,bshe->bhde', kb * k_decay[None, :, :, None], vb)
                return (S_new, o_intra + o_inter)
            S0 = jnp.zeros((b, h, d, d), dtype=q.dtype)
            S_final, oc = jax.lax.scan(step, S0, (qc, kc, vc))
            out = jnp.moveaxis(oc, 0, 1).reshape(b, n, h, d)
            return (out, S_final)

        def group_rmsnorm_fused_gate(o, gate, w, num_heads):
            b, n, d = o.shape
            hd = d // num_heads
            o = o * jax.nn.sigmoid(gate)
            og = o.reshape(b, n, num_heads, hd)
            og = og * jax.lax.rsqrt(jnp.mean(og * og, axis=-1, keepdims=True) + EPS)
            return og.reshape(b, n, d) * w
        b, n, d = x.shape
        H = log_decay.shape[0]
        hd = d // H
        q = jax.nn.silu(jnp.einsum('bnd,de->bne', x, Wq).reshape(b, n, H, hd))
        k = jax.nn.silu(jnp.einsum('bnd,de->bne', x, Wk).reshape(b, n, H, hd))
        v = jax.nn.silu(jnp.einsum('bnd,de->bne', x, Wv).reshape(b, n, H, hd))
        o, _ = lightning_attn(q, k, v, log_decay)
        o = o.reshape(b, n, d)
        gate = jnp.einsum('bnk,kd->bnd', jnp.einsum('bnd,dk->bnk', x, Wg1), Wg2)
        o = group_rmsnorm_fused_gate(o, gate, norm_w, H)
        return jnp.einsum('bnd,de->bne', o, Wo)

    def _L0_ffn_ref(input1, input2, scale, scale1):
        import jax, jax.numpy as jnp
        import numpy as np
        FP8 = jnp.float8_e4m3fn
        q1 = (input1 * scale).astype(FP8)
        q2 = (input2 * scale1).astype(FP8)
        d1 = q1.astype(jnp.float32) * (1.0 / scale)
        d2 = q2.astype(jnp.float32) * (1.0 / scale1)
        return jnp.einsum('bmk,kn->bmn', d1, d2)
    x = L0_attn_x
    xn = _layernorm(x, axis=-1)
    s = _L0_attn_ref(xn, L0_attn_log_decay, L0_attn_Wq, L0_attn_Wk, L0_attn_Wv, L0_attn_Wo, L0_attn_Wg1, L0_attn_Wg2, L0_attn_norm_w)
    g = _silu(_L0_ffn_ref(xn, L0_ffn_input2, L0_ffn_scale, L0_ffn_scale1))
    x = x + s * g
    return x

_drawn_inputs = setup_inputs


def setup_inputs(seed=0):
    import zlib

    import numpy as np

    out = dict(_drawn_inputs(seed))
    spreads = {'L0_attn_norm_w': (1.0, 0.2)}
    factors = {}
    for name, (base, spread) in spreads.items():
        noise = np.random.default_rng([zlib.crc32(name.encode()), seed]).standard_normal(out[name].shape)
        drawn = base * np.exp(spread * noise) if base else spread * noise
        out[name] = jnp.asarray(drawn.astype(out[name].dtype))
    for name, factor in factors.items():
        out[name] = (out[name] * factor).astype(out[name].dtype)
    return out
```

```python
from contextlib import ExitStack

import concourse.bass as bass
from concourse import mybir

F32 = mybir.dt.float32
F32R = mybir.dt.float32r
BF16 = mybir.dt.bfloat16
I32 = mybir.dt.int32
ALU = mybir.AluOpType
ACT = mybir.ActivationFunctionType
AX_X = mybir.AxisListType.X

P = 128
EPS = 1e-5


def layer_kernel(nc, x, log_decay, Wq, Wk, Wv, Wo, Wg1, Wg2, norm_w, W2, scale, scale1, out):
    B, N, D = x.shape
    H = log_decay.shape[0]
    E = D // H
    NB = N // P
    G = B * NB
    KH = D // P
    HH = H // KH
    C = P // 2
    GR = Wg1.shape[1]
    Q0 = 2 * D
    NW = 3 * D + GR
    LOOPS = B - 1
    assert (P, NB, KH, HH, E, GR) == (128, 4, 2, 8, 16, 16)

    E4_MIN = 2.0 ** -6
    E4_MAGIC = 1.5 * 2.0 ** 20
    E4_OVER = (2.0 ** 127) / 232.0

    with ExitStack() as ctx:
        def sb(name, shape, dt=F32):
            return ctx.enter_context(nc.sbuf_tensor(name, shape, dt))

        def sem(name):
            return ctx.enter_context(nc.semaphore(name))

        x_sb = sb("x_sb", [P, G, D])
        w_f32 = sb("w_f32", [P, KH, NW])
        w_hi = sb("w_hi", [P, KH, NW], F32R)
        w_lo = sb("w_lo", [P, KH, NW], F32R)
        wo_f32 = sb("wo_f32", [P, KH, D])
        wo_scaled = sb("wo_scaled", [P, KH, D])
        wo_hi = sb("wo_hi", [P, KH, D], F32R)
        wo_lo = sb("wo_lo", [P, KH, D], F32R)
        nw_col = sb("nw_col", [P, KH])
        wg2_f32 = sb("wg2_f32", [P, D])
        wg2_hi = sb("wg2_hi", [P, D], F32R)
        wg2_stack = sb("wg2_stack", [P, D], F32R)
        w2_f32 = sb("w2_f32", [P, KH, D])
        w2_y = sb("w2_y", [P, KH, D])
        w2_m = sb("w2_m", [P, KH, D])
        w2_q = sb("w2_q", [P, KH, D], BF16)
        w2_nan = sb("w2_nan", [P, KH, D], BF16)
        w2_fp8 = sb("w2_fp8", [P, KH, D], BF16)
        scales = sb("scales", [P, 2])
        inv_scales = sb("inv_scales", [P, 2])
        descale = sb("descale", [P, 1])
        ld_row = sb("ld_row", [P, H])
        ld_col = sb("ld_col", [P, KH])
        ident = sb("ident", [P, P])
        ident_bf = sb("ident_bf", [P, P], BF16)
        ones_row = sb("ones_row", [P, P])
        lag = sb("lag", [P, P])
        lag_clamped = sb("lag_clamped", [P, P])
        decay_mask = sb("decay_mask", [P, 4, 4, 2, C])
        pos_row = sb("pos_row", [P, 2, C])
        q_decay = sb("q_decay", [P, KH, P])
        pos_col = sb("pos_col", [P, 1])
        pos_col64 = sb("pos_col64", [P, 1])
        k_logdecay = sb("k_logdecay", [P, H])
        k_decay = sb("k_decay", [P, H])
        chunk_decay = sb("chunk_decay", [P, KH])
        state_decay = sb("state_decay", [P, KH, C])
        own_head = sb("own_head", [P, P])
        even_cols = sb("even_cols", [P, 4])
        head_parity = sb("head_parity", [P, 2])
        minus_half = sb("minus_half", [P, H])
        eps_col = sb("eps_col", [P, 1])

        bn6 = sb("bn6", [P, 2, 6])
        mean_var = sb("mean_var", [P, 2, 2])
        var_eps = sb("var_eps", [P, 2, 1])
        rstd = sb("rstd", [P, 2, 1])
        xn = sb("xn", [P, 2, D])
        e4_y = sb("e4_y", [P, D])
        e4_exp = sb("e4_exp", [P, D])
        e4_magic = sb("e4_magic", [P, D])
        e4_sum = sb("e4_sum", [P, D])
        e4_q = sb("e4_q", [P, D], BF16)
        e4_nan = sb("e4_nan", [P, D], BF16)
        xq = sb("xq", [P, 2, D], BF16)
        xT_hi = sb("xT_hi", [P, KH, P], F32R)
        xT_lo = sb("xT_lo", [P, KH, P], F32R)
        xqT = sb("xqT", [P, KH, P], BF16)
        kv = sb("kv", [P, 2, 2 * D])
        kd = sb("kd", [P, 2, D])
        q = sb("q", [P, D])
        g1_stack = sb("g1_stack", [P, P])
        g1T = sb("g1T", [P, P], F32R)
        kT = sb("kT", [P, 2, KH, P])
        qT = sb("qT", [P, 2, KH, 2, P])
        qdT = sb("qdT", [P, 2, KH, P])
        gate_tanh = sb("gate_tanh", [P, 2, D])
        ffn_silu = sb("ffn_silu", [P, 4, D])
        probs = sb("probs", [P, 4, 4, 2 * C])
        state = sb("state", [P, KH, C])
        state_kept = sb("state_kept", [P, KH, C])
        state_c0 = sb("state_c0", [P, 2, KH, P])
        state_c1 = sb("state_c1", [P, KH, P])
        og = sb("og", [P, D])
        og_sq = sb("og_sq", [P, D])
        og_sum = sb("og_sum", [P, H])
        og_var = sb("og_var", [P, H])
        og_rs = sb("og_rs", [P, H])
        on = sb("on", [P, D])
        oT_hi = sb("oT_hi", [P, KH, P], F32R)
        oT_lo = sb("oT_lo", [P, KH, P], F32R)
        sg = sb("sg", [P, D])
        y = sb("y", [P, 2, D])

        def bank(name):
            return ctx.enter_context(nc.psum_tensor(name, [P, 512], F32))

        b_score = [bank("b_score0"), bank("b_score1")]
        b_kv = bank("b_kv")
        b_qg = bank("b_qg")
        b_xo = bank("b_xo")
        b_qk = bank("b_qk")
        b_gate = bank("b_gate")
        b_att = bank("b_att")
        ps_xT = b_xo[:, 0:D].rearrange("p (k t) -> p k t", k=KH)
        ps_oT = ps_xT
        ps_out = b_xo[:, D:2 * D]
        ps_xqT = b_gate[:, 0:P].bitcast(BF16).rearrange("p (k t) -> p k t", k=KH)
        ps_g1T = b_gate[:, 0:P]
        ps_gate = b_gate[:, 0:D]
        ps_ffn = b_gate[:, D:2 * D]
        ps_qT = b_qk[:, 0:D].rearrange("p (k t) -> p k t", k=KH)
        ps_kT = b_qk[:, D:2 * D].rearrange("p (k t) -> p k t", k=KH)
        ps_state = b_att[:, 0:KH * C].rearrange("p (k c) -> p k c", k=KH)
        ps_o = b_att[:, D:2 * D]

        s_x = sem("x_loaded")
        s_w = sem("w_loaded")
        s_w2 = sem("w2_loaded")
        s_small = sem("small_loaded")
        s_wo = sem("wo_loaded")
        s_pool = sem("pool_constants")
        s_dvec = sem("dve_constants")
        s_actc = sem("act_constants")
        s_whi = sem("w_hi_ready")
        s_wlo = sem("w_lo_ready")
        s_g2w = sem("wg2_loaded")
        s_g2 = sem("wg2_stack_ready")
        s_woready = sem("wo_parts_ready")
        s_w2q = sem("w2_quant_steps")
        s_bn = sem("bn_ready")
        s_mv = sem("mean_var_ready")
        s_ve = sem("var_eps_ready")
        s_rstd = sem("rstd_ready")
        s_xn = sem("xn_ready")
        s_y4 = sem("e4_y_ready")
        s_exp = sem("e4_exp_ready")
        s_e4 = sem("e4_magic_ready")
        s_nan = sem("e4_nan_ready")
        s_e4p = sem("e4_pool_steps")
        s_xq = sem("xq_ready")
        s_xTps = sem("xT_in_psum")
        s_xqTps = sem("xqT_in_psum")
        s_xThi = sem("xT_hi_ready")
        s_xTlo = sem("xT_lo_ready")
        s_xqT = sem("xqT_ready")
        s_kvps = sem("kv_in_psum")
        s_qgps = sem("qg_in_psum")
        s_kv = sem("kv_ready")
        s_q = sem("q_ready")
        s_kd = sem("kd_ready")
        s_g1hi = sem("g1_hi_ready")
        s_g1lo = sem("g1_lo_ready")
        s_g1Tps = sem("g1T_in_psum")
        s_g1T = sem("g1T_ready")
        s_ffnps = sem("ffn_in_psum")
        s_ffn = sem("ffn_silu_ready")
        s_gateps = sem("gate_in_psum")
        s_gate = sem("gate_tanh_ready")
        s_qkTps = sem("qkT_in_psum")
        s_qkT = sem("qkT_ready")
        s_qd = sem("qdT_ready")
        s_score = sem("scores_in_psum")
        s_probs = sem("probs_ready")
        s_kvs = sem("state_step_in_psum")
        s_state = sem("state_ready")
        s_sx = sem("state_masked_ready")
        s_kept = sem("state_kept_ready")
        s_ops = sem("o_in_psum")
        s_og = sem("og_ready")
        s_sq = sem("og_sq_ready")
        s_sum = sem("og_sum_ready")
        s_var = sem("og_var_ready")
        s_rs = sem("og_rs_ready")
        s_on = sem("on_ready")
        s_oTps = sem("oT_in_psum")
        s_oThi = sem("oT_hi_ready")
        s_oTlo = sem("oT_lo_ready")
        s_outps = sem("out_in_psum")
        s_sg = sem("sg_ready")
        s_y = sem("y_ready")
        s_stored = sem("y_stored")

        x_v = x.rearrange("b (c p) d -> p (b c) d", p=P)
        out_v = out.rearrange("b (c p) d -> (b c) p d", p=P)

        def need(eng, s, v):
            if not isinstance(v, int) or v > 0:
                eng.wait_ge(s, v)

        def steps(program, prologue):
            def run(eng):
                prologue(eng)
                for j in range(2):
                    program(eng, 0, j)
                with eng.Fori(0, LOOPS) as i:
                    for j in range(2, NB + 2):
                        program(eng, i, j)
                for j in range(2, NB):
                    program(eng, LOOPS, j)
            return run

        def num(i, j):
            return NB * i + j

        def known(i, j):
            return not isinstance(i, int) or NB * i + j in range(G)

        def state_no(i, j, c):
            return (2 * NB - 1) * (i + j // NB) + 2 * (j % NB) + c

        def kept_no(i, j, c):
            return (2 * NB - 2) * (i + j // NB) + 2 * (j % NB) + c

        block = ctx.enter_context(nc.Block())

        @block.sync
        def _(sp):
            def prologue(sp):
                lots = [(0, 1), (1, NB)] + [(NB * b, NB * b + NB) for b in range(1, B)]
                for n, (a, b) in enumerate(lots):
                    need(sp, s_x, 16 * n)
                    sp.dma_start(x_sb[:, a:b, :], x_v[:, a:b, :]).then_inc(s_x, 16)

            def store(sp, i, j):
                if not known(i, j - 1):
                    return
                sp.wait_ge(s_y, num(i, j))
                dst = out_v[num(i, j - 1)] if isinstance(i, int) else out_v[bass.ds(num(i, j - 1), 1)].rearrange("a p d -> (a p) d")
                sp.dma_start(dst, y[:, (j - 1) % 2, :]).then_inc(s_stored, 16)

            steps(store, prologue)(sp)
            store(sp, LOOPS, NB)
            sp.wait_ge(s_stored, 16 * G)

        @block.gpsimd
        def _(pool):
            g = nc.gpsimd

            def norm_factor(i, j):
                u = j % 2
                pool.wait_ge(s_mv, num(i, j) + 1)
                need(pool, s_xn, num(i, j) - 1)
                g.tensor_tensor(var_eps[:, u], mean_var[:, u, 1:2], eps_col[:], ALU.add).then_inc(s_ve, 1)
                pool.wait_ge(s_ve, num(i, j) + 1)
                g.tensor_tensor(rstd[:, u], var_eps[:, u], minus_half[:, 0:1], ALU.pow).then_inc(s_rstd, 1)

            def scale_y(i, j):
                pool.wait_ge(s_xn, num(i, j) + 1)
                need(pool, s_e4p, 2 * num(i, j))
                g.tensor_tensor(e4_y[:], xn[:, j % 2], scales[:, 0:1].broadcast_to([P, D]), ALU.mult).then_inc(s_y4, 1)

            def round_y(i, j):
                base = 2 * num(i, j)
                pool.wait_ge(s_e4, num(i, j) + 1)
                g.tensor_tensor(e4_sum[:], e4_y[:], e4_magic[:], ALU.add).then_inc(s_e4p, 1)
                pool.wait_ge(s_e4p, base + 1)
                need(pool, s_xq, num(i, j))
                g.tensor_tensor(e4_q[:], e4_sum[:], e4_magic[:], ALU.subtract).then_inc(s_e4p, 1)

            def put_nan(i, j):
                pool.wait_ge(s_nan, num(i, j) + 1)
                need(pool, s_xqTps, num(i, j) - 1)
                g.tensor_tensor(xq[:, j % 2], e4_q[:], e4_nan[:], ALU.add).then_inc(s_xq, 1)

            def decay_k(i, j):
                u = j % 2
                pool.wait_ge(s_kv, num(i, j) + 1)
                need(pool, s_ops, num(i, j) - 1)
                g.tensor_tensor(kd[:, u].rearrange("p (h e) -> p h e", h=H),
                                kv[:, u, 0:D].rearrange("p (h e) -> p h e", h=H),
                                k_decay[:].unsqueeze(2).broadcast_to([P, H, E]), ALU.mult).then_inc(s_kd, 1)

            def spread_state(i, j, c):
                if j % NB == NB - 1 and c == 1:
                    return
                made = state_no(i, j, c) + 1
                pool.wait_ge(s_state, made)
                dst = state_c1 if c == 0 else state_c0[:, (j + 1) % 2]
                need(pool, s_ops, num(i, j) if c == 0 else num(i, j) - 1)
                g.tensor_tensor(dst[:].rearrange("p k (b c) -> p k b c", b=2),
                                state[:].unsqueeze(2).broadcast_to([P, KH, 2, C]),
                                own_head[:].rearrange("p (b c) -> p b c", b=2).unsqueeze(1).broadcast_to([P, KH, 2, C]),
                                ALU.mult).then_inc(s_sx, 1)
                if not (j % NB == NB - 1 and c == 0):
                    g.tensor_tensor(state_kept[:], state[:], state_decay[:], ALU.mult).then_inc(s_kept, 1)

            def square_o(i, j):
                pool.wait_ge(s_og, num(i, j) + 1)
                need(pool, s_sum, num(i, j))
                g.tensor_tensor(og_sq[:], og[:], og[:], ALU.mult).then_inc(s_sq, 1)

            def head_norm(i, j):
                pool.wait_ge(s_var, num(i, j) + 1)
                g.tensor_tensor(og_rs[:], og_var[:], minus_half[:], ALU.pow).then_inc(s_rs, 1)
                pool.wait_ge(s_rs, num(i, j) + 1)
                need(pool, s_oTps, num(i, j))
                g.tensor_tensor(on[:].rearrange("p (h e) -> p h e", h=H), og[:].rearrange("p (h e) -> p h e", h=H),
                                og_rs[:].unsqueeze(2).broadcast_to([P, H, E]), ALU.mult).then_inc(s_on, 1)

            def add_x(i, j):
                pool.wait_ge(s_sg, num(i, j) + 1)
                need(pool, s_stored, 16 * num(i, j))
                xs = x_sb[:, num(i, j), :] if isinstance(i, int) else x_sb[:, bass.ds(num(i, j), 1), :].rearrange("p a d -> p (a d)")
                g.tensor_tensor(y[:, j % 2, :], sg[:], xs, ALU.add).then_inc(s_y, 1)

            def prologue(pool):
                g.memset(minus_half[:], -0.5)
                g.memset(eps_col[:], EPS).then_inc(s_pool, 1)
                g.memset(ident[:], 0.0).then_inc(s_pool, 1)
                g.memset(ones_row[:], 1.0).then_inc(s_pool, 1)
                g.memset(wg2_f32[:], 0.0).then_inc(s_pool, 1)
                g.memset(g1_stack[:], 0.0).then_inc(s_pool, 1)
                g.memset(wg2_stack[:].bitcast(F32), 0.0).then_inc(s_pool, 1)
                pool.wait_ge(s_pool, 6)
                for r in range(4):
                    pool.dma_start(wg2_f32[32 * r:32 * r + GR, :], Wg2).then_inc(s_g2w, 16)
                g.affine_select(out=ident[:], in_=ident[:], compare_op=ALU.not_equal, fill=1.0, base=0,
                                pattern=[[-1, P]], channel_multiplier=1).then_inc(s_pool, 1)
                g.iota(lag[:], pattern=[[1, P]], base=0, channel_multiplier=-1, allow_small_or_imprecise_dtypes=True).then_inc(s_pool, 1)
                g.iota(pos_row[:], pattern=[[0, 2], [1, C]], base=1, channel_multiplier=0, allow_small_or_imprecise_dtypes=True).then_inc(s_pool, 1)
                g.iota(pos_col64[:], pattern=[[0, 1]], base=2 * C - 1, channel_multiplier=-1, allow_small_or_imprecise_dtypes=True).then_inc(s_pool, 1)
                pool.wait_ge(s_pool, 10)
                g.tensor_scalar(pos_col[0:C], pos_col64[0:C], -float(C), 1.0, ALU.add, ALU.mult).then_inc(s_pool, 1)
                pool.wait_ge(s_pool, 11)
                g.tensor_scalar(pos_col[C:P], pos_col64[C:P], 1.0, 0.0, ALU.mult, ALU.add).then_inc(s_pool, 1)
                pool.wait_ge(s_pool, 12)
                g.affine_select(out=own_head[:].rearrange("p (h e) -> p h e", h=HH), in_=ones_row[:].rearrange("p (h e) -> p h e", h=HH),
                                compare_op=ALU.is_ge, fill=0.0, base=0, pattern=[[-E, HH], [0, E]], channel_multiplier=1).then_inc(s_pool, 1)
                pool.wait_ge(s_pool, 13)
                g.affine_select(out=own_head[:].rearrange("p (h e) -> p h e", h=HH), in_=own_head[:].rearrange("p (h e) -> p h e", h=HH),
                                compare_op=ALU.is_ge, fill=0.0, base=E - 1, pattern=[[E, HH], [0, E]], channel_multiplier=-1).then_inc(s_pool, 1)
                g.affine_select(out=even_cols[:], in_=ones_row[:, 0:4], compare_op=ALU.is_ge, fill=0.0, base=0,
                                pattern=[[-2 * E, 4]], channel_multiplier=1).then_inc(s_pool, 1)
                pool.wait_ge(s_pool, 15)
                g.affine_select(out=even_cols[:], in_=even_cols[:], compare_op=ALU.is_ge, fill=0.0, base=E - 1,
                                pattern=[[2 * E, 4]], channel_multiplier=-1).then_inc(s_pool, 1)
                norm_factor(0, 0)
                pool.wait_ge(s_small, 80)
                scale_y(0, 0)
                norm_factor(0, 1)
                round_y(0, 0)
                put_nan(0, 0)
                pool.wait_ge(s_actc, H)
                dm = decay_mask[:].rearrange("p r i b c -> p (r i) (b c)")
                g.affine_select(out=dm, in_=dm, compare_op=ALU.is_ge, fill=0.0, base=0,
                                pattern=[[0, H], [1, P]], channel_multiplier=-1).then_inc(s_pool, 1)
                pool.wait_ge(s_pool, 17)
                g.memset(dm[0:C, :, C:P], 0.0).then_inc(s_pool, 1)
                pool.wait_ge(s_actc, H + 4)
                scale_y(0, 1)
                round_y(0, 1)
                put_nan(0, 1)
                decay_k(0, 0)

            def step(pool, i, j):
                if known(i, j + 2):
                    norm_factor(i, j + 2)
                spread_state(i, j, 0)
                if known(i, j + 2):
                    scale_y(i, j + 2)
                spread_state(i, j, 1)
                if known(i, j + 2):
                    round_y(i, j + 2)
                if known(i, j + 1):
                    decay_k(i, j + 1)
                if known(i, j + 2):
                    put_nan(i, j + 2)
                square_o(i, j)
                if known(i, j - 1):
                    add_x(i, j - 1)
                head_norm(i, j)

            steps(step, prologue)(pool)
            add_x(LOOPS, NB - 1)

        @block.scalar
        def _(act):
            a = nc.scalar

            def high_xT(i, j):
                act.wait_ge(s_xTps, num(i, j) + 1)
                need(act, s_qgps, num(i, j))
                a.activation(xT_hi[:], ps_xT, ACT.Copy).then_inc(s_xThi, 1)
                act.wait_ge(s_xqTps, num(i, j) + 1)
                need(act, s_ffnps, num(i, j))
                a.activation(xqT[:], ps_xqT, ACT.Copy).then_inc(s_xqT, 1)

            def silu_kv(i, j):
                act.wait_ge(s_kvps, num(i, j) + 1)
                need(act, s_ops, num(i, j) - 1)
                need(act, s_kd, num(i, j) - 1)
                a.activation(kv[:, j % 2], b_kv[:], ACT.Silu).then_inc(s_kv, 1)

            def silu_q(i, j):
                act.wait_ge(s_qgps, num(i, j) + 1)
                need(act, s_qkTps, num(i, j))
                a.activation(q[:], b_qg[:, 0:D], ACT.Silu).then_inc(s_q, 1)
                need(act, s_g1Tps, num(i, j))
                a.activation(g1_stack[:, 0:64].bitcast(F32R).rearrange("p (r c) -> p r c", r=2)[:, :, 0:GR],
                             b_qg[:, D:D + GR].unsqueeze(1).broadcast_to([P, 2, GR]), ACT.Copy).then_inc(s_g1hi, 1)

            def silu_ffn(i, j):
                act.wait_ge(s_ffnps, num(i, j) + 1)
                need(act, s_sg, num(i, j) - 2)
                a.activation(ffn_silu[:, j % 4], ps_ffn, ACT.Silu, scale=descale[:, 0:1]).then_inc(s_ffn, 1)

            def copy_g1T(i, j):
                act.wait_ge(s_g1Tps, num(i, j) + 1)
                need(act, s_gateps, num(i, j))
                a.activation(g1T[:], ps_g1T, ACT.Copy).then_inc(s_g1T, 1)

            def copy_qkT(i, j):
                u = j % 2
                act.wait_ge(s_qkTps, num(i, j) + 1)
                need(act, s_score, 4 * (num(i, j) - 1))
                a.activation(kT[:, u], ps_kT, ACT.Copy).then_inc(s_qkT, 1)
                for par in range(2):
                    a.activation(qT[:, u, :, par, :], ps_qT, ACT.Copy, scale=head_parity[:, par:par + 1]).then_inc(s_qkT, 1)

            def gate(i, j):
                act.wait_ge(s_gateps, num(i, j) + 1)
                need(act, s_og, num(i, j) - 1)
                a.activation(gate_tanh[:, j % 2], ps_gate, ACT.Tanh, scale=0.5).then_inc(s_gate, 1)

            def high_oT(i, j):
                act.wait_ge(s_oTps, num(i, j) + 1)
                need(act, s_outps, num(i, j))
                a.activation(oT_hi[:], ps_oT, ACT.Copy).then_inc(s_oThi, 1)

            def front(i, j):
                high_xT(i, j)
                silu_kv(i, j)
                silu_q(i, j)
                silu_ffn(i, j)

            def front_late(i, j):
                copy_g1T(i, j)
                copy_qkT(i, j)
                gate(i, j)

            def prologue(act):
                for kk in range(KH):
                    act.dma_start(w_f32[:, kk, 0:D], Wk[kk * P:kk * P + P, :]).then_inc(s_w, 16)
                    act.dma_start(w_f32[:, kk, D:2 * D], Wv[kk * P:kk * P + P, :]).then_inc(s_w, 16)
                    act.dma_start(w_f32[:, kk, Q0:Q0 + D], Wq[kk * P:kk * P + P, :]).then_inc(s_w, 16)
                    act.dma_start(w_f32[:, kk, 3 * D:NW], Wg1[kk * P:kk * P + P, :]).then_inc(s_w, 16)
                act.dma_start(ld_row[:], log_decay.unsqueeze(0).broadcast_to([P, H])).then_inc(s_small, 16)
                for half in range(KH):
                    act.dma_start(ld_col[:, half:half + 1],
                                  log_decay[half * HH:half * HH + HH].unsqueeze(1).broadcast_to([HH, E])).then_inc(s_small, 16)
                act.dma_start(scales[:, 0:1], scale.unsqueeze(0).broadcast_to([P, 1])).then_inc(s_small, 16)
                act.dma_start(scales[:, 1:2], scale1.unsqueeze(0).broadcast_to([P, 1])).then_inc(s_small, 16)
                act.dma_start(w2_f32[:], W2.rearrange("(k p) n -> p k n", p=P)).then_inc(s_w2, 16)
                act.dma_start(wo_f32[:], Wo.rearrange("(k p) n -> p k n", p=P)).then_inc(s_wo, 16)
                for kk in range(KH):
                    act.dma_start(nw_col[:, kk:kk + 1], norm_w[kk * P:kk * P + P].unsqueeze(1)).then_inc(s_wo, 16)
                act.wait_ge(s_small, 80)
                act.wait_ge(s_dvec, 1)
                for r in range(4):
                    for k in range(4):
                        h = HH * (k // 2) + 2 * r + k % 2
                        a.activation(decay_mask[:, r, k].rearrange("p b c -> p (b c)"), lag_clamped[:], ACT.Exp,
                                     scale=ld_row[:, h:h + 1]).then_inc(s_actc, 1)
                for half in range(KH):
                    a.activation(q_decay[:, half], pos_row[:].rearrange("p b c -> p (b c)"), ACT.Exp,
                                 scale=ld_col[:, half:half + 1]).then_inc(s_actc, 1)
                act.wait_ge(s_dvec, 2)
                a.activation(k_decay[:], k_logdecay[:], ACT.Exp).then_inc(s_actc, 1)
                a.activation(chunk_decay[:], ld_col[:], ACT.Exp, scale=float(C)).then_inc(s_actc, 1)
                act.wait_ge(s_w, 128)
                for kk in range(KH):
                    a.activation(w_hi[:, kk], w_f32[:, kk], ACT.Copy).then_inc(s_whi, 1)
                act.wait_ge(s_dvec, 6)
                front(0, 0)
                front_late(0, 0)

            def step(act, i, j):
                if known(i, j + 1):
                    front(i, j + 1)
                if known(i, j - 1):
                    high_oT(i, j - 1)
                if known(i, j + 1):
                    front_late(i, j + 1)

            steps(step, prologue)(act)
            high_oT(LOOPS, NB - 1)

        @block.vector
        def _(dve):
            v = nc.vector

            def stats(i, j):
                u = j % 2
                if isinstance(i, int) and NB * i + j == 0:
                    dve.wait_ge(s_x, 16)
                else:
                    dve.wait_ge(s_x, 16 * (i + j // NB) + 32)
                xs = x_sb[:, num(i, j), :] if isinstance(i, int) else x_sb[:, bass.ds(num(i, j), 1), :].rearrange("p a d -> p (a d)")
                v.bn_stats(bn6[:, u], xs).then_inc(s_bn, 1)

            def aggregate_waits(i, j):
                dve.wait_ge(s_bn, num(i, j) + 1)
                need(dve, s_ve, num(i, j) - 1)

            def aggregate(i, j):
                u = j % 2
                v.bn_aggr(mean_var[:, u], bn6[:, u]).then_inc(s_mv, 1)

            def normalise(i, j):
                u = j % 2
                dve.wait_ge(s_mv, num(i, j) + 1)
                dve.wait_ge(s_rstd, num(i, j) + 1)
                need(dve, s_xTps, num(i, j) - 1)
                need(dve, s_y4, num(i, j) - 1)
                xs = x_sb[:, num(i, j), :] if isinstance(i, int) else x_sb[:, bass.ds(num(i, j), 1), :].rearrange("p a d -> p (a d)")
                v.tensor_scalar(xn[:, u], xs, mean_var[:, u, 0:1], rstd[:, u, 0:1], ALU.subtract, ALU.mult).then_inc(s_xn, 1)

            def exponent(i, j):
                dve.wait_ge(s_y4, num(i, j) + 1)
                need(dve, s_e4p, 2 * num(i, j))
                v.tensor_scalar(e4_exp[:].bitcast(I32), e4_y[:].bitcast(I32), 0x7F800000, None, ALU.bitwise_and).then_inc(s_exp, 1)
                dve.wait_ge(s_exp, num(i, j) + 1)
                v.tensor_scalar(e4_magic[:], e4_exp[:], E4_MIN, E4_MAGIC, ALU.max, ALU.mult).then_inc(s_e4, 1)

            def find_nan(i, j):
                dve.wait_ge(s_e4p, 2 * (num(i, j) + 1))
                need(dve, s_xq, num(i, j))
                v.tensor_scalar(e4_nan[:], e4_q[:], E4_OVER, 0.0, ALU.mult, ALU.mult).then_inc(s_nan, 1)

            def low_xT(i, j):
                dve.wait_ge(s_xThi, num(i, j) + 1)
                need(dve, s_qgps, num(i, j))
                v.tensor_tensor(xT_lo[:], ps_xT, xT_hi[:].bitcast(F32), ALU.subtract).then_inc(s_xTlo, 1)

            def low_g1(i, j):
                dve.wait_ge(s_g1hi, num(i, j) + 1)
                v.tensor_tensor(g1_stack[:, 64:128].bitcast(F32R).rearrange("p (r c) -> p r c", r=2)[:, :, 0:GR],
                                b_qg[:, D:D + GR].unsqueeze(1).broadcast_to([P, 2, GR]),
                                g1_stack[:, 0:64].rearrange("p (r c) -> p r c", r=2)[:, :, 0:GR],
                                ALU.subtract).then_inc(s_g1lo, 1)

            def mask(i, j, r):
                dve.wait_ge(s_score, 4 * num(i, j) + r + 1)
                need(dve, s_ops, num(i, j))
                v.tensor_tensor(probs[:, r].rearrange("p i (b c) -> p i b c", b=2),
                                b_score[r % 2][:, 0:4 * C].rearrange("p (i c) -> p i c", i=4).unsqueeze(2).broadcast_to([P, 4, 2, C]),
                                decay_mask[:, r], ALU.mult).then_inc(s_probs, 1)

            def add_state(i, j, c):
                if j % NB == NB - 1 and c == 1:
                    return
                dve.wait_ge(s_kvs, state_no(i, j, c) + 1)
                if j % NB == 0 and c == 0:
                    need(dve, s_sx, state_no(i, j, c))
                    v.tensor_copy(state[:], ps_state).then_inc(s_state, 1)
                else:
                    dve.wait_ge(s_kept, kept_no(i, j, c))
                    v.tensor_tensor(state[:], ps_state, state_kept[:], ALU.add).then_inc(s_state, 1)

            def decay_q(i, j):
                dve.wait_ge(s_qkT, 3 * (num(i, j) + 1))
                need(dve, s_ops, num(i, j) - 1)
                v.tensor_tensor(qdT[:, j % 2], ps_qT, q_decay[:], ALU.mult).then_inc(s_qd, 1)

            def gate_o(i, j):
                dve.wait_ge(s_ops, num(i, j) + 1)
                dve.wait_ge(s_gate, num(i, j) + 1)
                need(dve, s_on, num(i, j))
                v.scalar_tensor_tensor(out=og[:], in0=gate_tanh[:, j % 2], scalar=1.0, in1=ps_o,
                                       op0=ALU.add, op1=ALU.mult).then_inc(s_og, 1)

            def sum_heads(i, j):
                dve.wait_ge(s_sq, num(i, j) + 1)
                v.tensor_reduce(og_sum[:], og_sq[:].rearrange("p (h e) -> p h e", h=H), AX_X, ALU.add).then_inc(s_sum, 1)
                dve.wait_ge(s_sum, num(i, j) + 1)
                need(dve, s_rs, num(i, j))
                v.tensor_scalar(og_var[:], og_sum[:], 1.0 / E, 4.0 * EPS, ALU.mult, ALU.add).then_inc(s_var, 1)

            def low_oT(i, j):
                dve.wait_ge(s_oThi, num(i, j) + 1)
                need(dve, s_outps, num(i, j))
                v.tensor_tensor(oT_lo[:], ps_oT, oT_hi[:].bitcast(F32), ALU.subtract).then_inc(s_oTlo, 1)

            def product(i, j):
                dve.wait_ge(s_outps, num(i, j) + 1)
                dve.wait_ge(s_ffn, num(i, j) + 1)
                need(dve, s_y, num(i, j))
                v.tensor_tensor(sg[:], ps_out, ffn_silu[:, j % 4], ALU.mult).then_inc(s_sg, 1)

            def prologue(dve):
                stats(0, 0)
                aggregate_waits(0, 0)
                aggregate(0, 0)
                dve.wait_ge(s_pool, 12)
                v.tensor_scalar(lag_clamped[:], lag[:], 0.0, None, ALU.max).then_inc(s_dvec, 1)
                normalise(0, 0)
                stats(0, 1)
                aggregate_waits(0, 1)
                aggregate(0, 1)
                dve.wait_ge(s_small, 80)
                v.tensor_scalar(k_logdecay[:], ld_row[:], pos_col[:, 0:1], None, ALU.mult).then_inc(s_dvec, 1)
                v.tensor_copy(ident_bf[:], ident[:]).then_inc(s_dvec, 1)
                v.reciprocal(inv_scales[:], scales[:]).then_inc(s_dvec, 1)
                dve.wait_ge(s_dvec, 4)
                v.tensor_scalar(descale[:], inv_scales[:, 0:1], inv_scales[:, 1:2], None, ALU.mult).then_inc(s_dvec, 1)
                dve.wait_ge(s_pool, 16)
                v.tensor_reduce(head_parity[:, 0:1], even_cols[:], AX_X, ALU.add).then_inc(s_dvec, 1)
                dve.wait_ge(s_dvec, 6)
                v.tensor_scalar(head_parity[:, 1:2], head_parity[:, 0:1], -1.0, 1.0, ALU.mult, ALU.add).then_inc(s_dvec, 1)
                exponent(0, 0)
                normalise(0, 1)
                find_nan(0, 0)
                for kk in range(KH):
                    dve.wait_ge(s_whi, kk + 1)
                    v.tensor_tensor(w_lo[:, kk], w_f32[:, kk], w_hi[:, kk].bitcast(F32), ALU.subtract).then_inc(s_wlo, 1)
                low_xT(0, 0)
                dve.wait_ge(s_w2, 16)
                v.tensor_scalar(w2_y[:], w2_f32[:], scales[:, 1:2], None, ALU.mult).then_inc(s_w2q, 1)
                dve.wait_ge(s_w2q, 1)
                v.tensor_scalar(w2_m[:].bitcast(I32), w2_y[:].bitcast(I32), 0x7F800000, None, ALU.bitwise_and).then_inc(s_w2q, 1)
                dve.wait_ge(s_w2q, 2)
                v.tensor_scalar(w2_f32[:], w2_m[:], E4_MIN, E4_MAGIC, ALU.max, ALU.mult).then_inc(s_w2q, 1)
                dve.wait_ge(s_w2q, 3)
                v.tensor_tensor(w2_m[:], w2_y[:], w2_f32[:], ALU.add).then_inc(s_w2q, 1)
                dve.wait_ge(s_w2q, 4)
                v.tensor_tensor(w2_q[:], w2_m[:], w2_f32[:], ALU.subtract).then_inc(s_w2q, 1)
                dve.wait_ge(s_w2q, 5)
                v.tensor_scalar(w2_nan[:], w2_q[:], E4_OVER, 0.0, ALU.mult, ALU.mult).then_inc(s_w2q, 1)
                dve.wait_ge(s_w2q, 6)
                v.tensor_tensor(w2_fp8[:], w2_q[:], w2_nan[:], ALU.add).then_inc(s_w2q, 1)
                low_g1(0, 0)
                dve.wait_ge(s_g2w, 64)
                dve.wait_ge(s_pool, 6)
                v.tensor_copy(wg2_hi[:], wg2_f32[:]).then_inc(s_g2, 1)
                dve.wait_ge(s_g2, 1)
                for r in range(4):
                    rows = slice(32 * r, 32 * r + GR)
                    if r % 2 == 0:
                        v.tensor_copy(wg2_stack[rows], wg2_f32[rows]).then_inc(s_g2, 1)
                    else:
                        v.tensor_tensor(wg2_stack[rows], wg2_f32[rows], wg2_hi[rows].bitcast(F32), ALU.subtract).then_inc(s_g2, 1)
                exponent(0, 1)
                find_nan(0, 1)
                dve.wait_ge(s_actc, H + 4)
                v.tensor_copy(state_decay[:], chunk_decay[:].unsqueeze(2).broadcast_to([P, KH, C])).then_inc(s_dvec, 1)
                decay_q(0, 0)
                dve.wait_ge(s_wo, 48)
                for kk in range(KH):
                    v.tensor_scalar(wo_scaled[:, kk], wo_f32[:, kk], nw_col[:, kk:kk + 1], None, ALU.mult).then_inc(s_woready, 1)
                dve.wait_ge(s_woready, 2)
                v.tensor_copy(wo_hi[:], wo_scaled[:]).then_inc(s_woready, 1)
                dve.wait_ge(s_woready, 3)
                v.tensor_tensor(wo_lo[:], wo_scaled[:], wo_hi[:].bitcast(F32), ALU.subtract).then_inc(s_woready, 1)
                dve.wait_ge(s_pool, 18)

            def step(dve, i, j):
                nxt, back, norm = known(i, j + 1), known(i, j - 1), known(i, j + 2)
                mask(i, j, 0)
                if norm:
                    stats(i, j + 2)
                    aggregate_waits(i, j + 2)
                if nxt:
                    low_xT(i, j + 1)
                if norm:
                    aggregate(i, j + 2)
                add_state(i, j, 0)
                mask(i, j, 1)
                if norm:
                    normalise(i, j + 2)
                add_state(i, j, 1)
                mask(i, j, 2)
                if nxt:
                    low_g1(i, j + 1)
                if norm:
                    exponent(i, j + 2)
                mask(i, j, 3)
                if back:
                    low_oT(i, j - 1)
                if nxt:
                    decay_q(i, j + 1)
                if norm:
                    find_nan(i, j + 2)
                gate_o(i, j)
                sum_heads(i, j)
                if back:
                    product(i, j - 1)

            steps(step, prologue)(dve)
            low_oT(LOOPS, NB - 1)
            product(LOOPS, NB - 1)

        @block.tensor
        def _(pe):
            t = nc.tensor

            def transpose_x(i, j):
                u = j % 2
                pe.wait_ge(s_xn, num(i, j) + 1)
                need(pe, s_sg, num(i, j) - 2)
                for kk in range(KH):
                    mm = t.transpose(ps_xT[:, kk, :], xn[:, u, kk * P:kk * P + P], ident[:])
                mm.then_inc(s_xTps, 1)
                pe.wait_ge(s_xq, num(i, j) + 1)
                need(pe, s_gate, num(i, j))
                for kk in range(KH):
                    mm = t.transpose(ps_xqT[:, kk, :], xq[:, u, kk * P:kk * P + P], ident_bf[:])
                mm.then_inc(s_xqTps, 1)

            def project(i, j, dst, a, b, s_done, s_free, free):
                pe.wait_ge(s_xThi, num(i, j) + 1)
                need(pe, s_free, free)
                for kk in range(KH):
                    t.matmul(dst, xT_hi[:, kk], w_hi[:, kk, a:b], start=(kk == 0), stop=False)
                for kk in range(KH):
                    t.matmul(dst, xT_hi[:, kk], w_lo[:, kk, a:b], start=False, stop=False)
                pe.wait_ge(s_xTlo, num(i, j) + 1)
                for kk in range(KH):
                    mm = t.matmul(dst, xT_lo[:, kk], w_hi[:, kk, a:b], start=False, stop=(kk == KH - 1))
                mm.then_inc(s_done, 1)

            def project_kv(i, j):
                project(i, j, b_kv[:, :], 0, 2 * D, s_kvps, s_kv, num(i, j))

            def project_qg(i, j):
                project(i, j, b_qg[:, 0:NW - Q0], Q0, NW, s_qgps, s_g1lo, num(i, j))

            def ffn(i, j):
                pe.wait_ge(s_xqT, num(i, j) + 1)
                for kk in range(KH):
                    mm = t.matmul(ps_ffn, xqT[:, kk], w2_fp8[:, kk], start=(kk == 0), stop=(kk == KH - 1))
                mm.then_inc(s_ffnps, 1)

            def transpose_g1(i, j):
                pe.wait_ge(s_g1lo, num(i, j) + 1)
                pe.wait_ge(s_ffn, num(i, j) + 1)
                t.transpose(ps_g1T, g1_stack[:], ident[:]).then_inc(s_g1Tps, 1)

            def transpose_qk(i, j):
                pe.wait_ge(s_kv, num(i, j) + 1)
                pe.wait_ge(s_q, num(i, j) + 1)
                need(pe, s_qd, num(i, j))
                for kk in range(KH):
                    t.transpose(ps_qT[:, kk, :], q[:, kk * P:kk * P + P], ident[:])
                for kk in range(KH):
                    mm = t.transpose(ps_kT[:, kk, :], kv[:, j % 2, kk * P:kk * P + P], ident[:])
                mm.then_inc(s_qkTps, 1)

            def gate(i, j):
                pe.wait_ge(s_g1T, num(i, j) + 1)
                t.matmul(ps_gate, g1T[:], wg2_stack[:], start=True, stop=True).then_inc(s_gateps, 1)

            def scores(i, j, r):
                u = j % 2
                if r == 0:
                    pe.wait_ge(s_qkT, 3 * (num(i, j) + 1))
                need(pe, s_probs, 4 * num(i, j) + r - 1)
                rows = slice(32 * r, 32 * r + 32)
                for half in range(KH):
                    for c in range(2):
                        mm = t.matmul(b_score[r % 2][c * C:c * C + C, half * 2 * C:(half + 1) * 2 * C],
                                      kT[rows, u, half, c * C:c * C + C], qT[rows, u, half, :, c * C:c * C + C],
                                      start=True, stop=True)
                mm.then_inc(s_score, 1)

            def state_waits(i, j, c):
                if c == 0:
                    pe.wait_ge(s_kd, num(i, j) + 1)
                    need(pe, s_og, num(i, j))
                else:
                    pe.wait_ge(s_state, state_no(i, j, 1))

            def state_step(i, j, c):
                if j % NB == NB - 1 and c == 1:
                    return
                u = j % 2
                rows = slice(c * C, c * C + C)
                for half in range(KH):
                    for b in range(2):
                        cols = slice(half * P + b * C, half * P + b * C + C)
                        mm = t.matmul(ps_state[b * C:b * C + C, half, :], kd[rows, u, cols],
                                      kv[rows, u, D + cols.start:D + cols.stop], start=True, stop=True)
                mm.then_inc(s_kvs, 1)

            def attend(i, j):
                u = j % 2
                first = j % NB == 0

                def from_state():
                    pe.wait_ge(s_qd, num(i, j) + 1)
                    pe.wait_ge(s_sx, state_no(i, j, 1))
                    for c in range(1 if first else 0, 2):
                        st = state_c0[:, u] if c == 0 else state_c1
                        for half in range(KH):
                            mm = t.matmul(ps_o[c * C:c * C + C, half * P:half * P + P], qdT[:, u, half, c * C:c * C + C],
                                          st[:, half, :], start=(half == 0 and not first), stop=False, skip_group_check=True)
                    return mm

                def from_chunk():
                    for r in range(4):
                        pe.wait_ge(s_probs, 4 * num(i, j) + r + 1)
                        for k in range(4):
                            h = HH * (k // 2) + 2 * r + k % 2
                            mm = t.matmul(ps_o[:, h * E:h * E + E], probs[:, r, k, :], kv[:, u, D + h * E:D + h * E + E],
                                          start=(first and r == 0 and k == 0), stop=(r == 3 and k == 3), skip_group_check=True)
                    return mm

                if j % NB == NB - 1:
                    pe.wait_ge(s_state, state_no(i, j, 1))
                else:
                    pe.wait_ge(s_state, state_no(i, j, 1) + 1)
                if first:
                    from_chunk()
                    mm = from_state()
                else:
                    from_state()
                    mm = from_chunk()
                mm.then_inc(s_ops, 1)

            def transpose_o(i, j):
                pe.wait_ge(s_on, num(i, j) + 1)
                if known(i, j + 2):
                    pe.wait_ge(s_xTlo, num(i, j) + 3)
                for kk in range(KH):
                    mm = t.transpose(ps_oT[:, kk, :], on[:, kk * P:kk * P + P], ident[:])
                mm.then_inc(s_oTps, 1)

            def project_o(i, j):
                pe.wait_ge(s_oTlo, num(i, j) + 1)
                parts = [(oT_hi, wo_hi), (oT_hi, wo_lo), (oT_lo, wo_hi)]
                for n, (lhs, rhs) in enumerate(parts):
                    for kk in range(KH):
                        mm = t.matmul(ps_out, lhs[:, kk], rhs[:, kk], start=(n == 0 and kk == 0), stop=(n == 2 and kk == KH - 1))
                mm.then_inc(s_outps, 1)

            def prologue(pe):
                pe.wait_ge(s_pool, 7)
                pe.wait_ge(s_dvec, 3)
                transpose_x(0, 0)
                pe.wait_ge(s_wlo, 2)
                project_kv(0, 0)
                project_qg(0, 0)
                pe.wait_ge(s_w2q, 7)
                ffn(0, 0)
                transpose_g1(0, 0)
                transpose_qk(0, 0)
                pe.wait_ge(s_g2, 5)
                gate(0, 0)
                pe.wait_ge(s_woready, 4)

            def step(pe, i, j):
                nxt, back = known(i, j + 1), known(i, j - 1)
                scores(i, j, 0)
                if nxt:
                    transpose_x(i, j + 1)
                state_waits(i, j, 0)
                scores(i, j, 1)
                state_step(i, j, 0)
                if nxt:
                    project_kv(i, j + 1)
                state_waits(i, j, 1)
                scores(i, j, 2)
                state_step(i, j, 1)
                if nxt:
                    project_qg(i, j + 1)
                    ffn(i, j + 1)
                scores(i, j, 3)
                if back:
                    transpose_o(i, j - 1)
                if nxt:
                    transpose_qk(i, j + 1)
                    transpose_g1(i, j + 1)
                attend(i, j)
                if nxt:
                    gate(i, j + 1)
                if back:
                    project_o(i, j - 1)

            steps(step, prologue)(pe)
            transpose_o(LOOPS, NB - 1)
            project_o(LOOPS, NB - 1)


_INS = ['L0_attn_x', 'L0_attn_log_decay', 'L0_attn_Wq', 'L0_attn_Wk', 'L0_attn_Wv', 'L0_attn_Wo', 'L0_attn_Wg1',
        'L0_attn_Wg2', 'L0_attn_norm_w', 'L0_ffn_input2', 'L0_ffn_scale', 'L0_ffn_scale1']
_OUTS = [((4, 512, 256), 'float32')]


def kernel(**inputs):
    import numpy as _np
    import concourse.bacc as _bacc
    from concourse import mybir as _mybir
    from concourse.bass_utils import run_bass_kernel_spmd as _run

    nc = _bacc.Bacc("TRN2", target_bir_lowering=False, num_devices=1)
    arrays, args = {}, []
    for name in _INS:
        a = _np.ascontiguousarray(inputs[name])
        if a.ndim == 0:
            a = a.reshape(1)
        arrays[f"in_{name}_dram"] = a
        args.append(nc.dram_tensor(f"in_{name}_dram", a.shape, _mybir.dt.from_np(a.dtype), kind="ExternalInput").ap())
    for i, (shape, dtype) in enumerate(_OUTS):
        dt = _mybir.dt.from_np(_np.dtype(dtype))
        args.append(nc.dram_tensor(f"out_{i}_dram", shape, dt, kind="ExternalOutput").ap())
    layer_kernel(nc, *args)
    r = _run(nc, [arrays], core_ids=[0])
    return r.results[0]["out_0_dram"]
```

```python
from contextlib import ExitStack

import concourse.bass as bass
from concourse import mybir

F32 = mybir.dt.float32
F32R = mybir.dt.float32r
BF16 = mybir.dt.bfloat16
I32 = mybir.dt.int32
ALU = mybir.AluOpType
ACT = mybir.ActivationFunctionType
AX_X = mybir.AxisListType.X

P = 128
EPS = 1e-5


def layer_kernel(nc, x, log_decay, Wq, Wk, Wv, Wo, Wg1, Wg2, norm_w, W2, scale, scale1, out):
    B, N, D = x.shape
    H = log_decay.shape[0]
    E = D // H
    NB = N // P
    G = B * NB
    KH = D // P
    HH = H // KH
    C = P // 2
    GR = Wg1.shape[1]
    Q0 = 2 * D
    NW = 3 * D + GR
    LOOPS = B - 1
    RS_STEPS = 12
    assert (P, NB, KH, HH, E, GR) == (128, 4, 2, 8, 16, 16)

    E4_MIN = 2.0 ** -6
    E4_MAGIC = 1.5 * 2.0 ** 20
    E4_OVER = (2.0 ** 127) / 232.0

    with ExitStack() as ctx:
        def sb(name, shape, dt=F32):
            return ctx.enter_context(nc.sbuf_tensor(name, shape, dt))

        def sem(name):
            return ctx.enter_context(nc.semaphore(name))

        x_sb = sb("x_sb", [P, G, D])
        w_f32 = sb("w_f32", [P, KH, NW])
        w_hi = sb("w_hi", [P, KH, NW], F32R)
        w_lo = sb("w_lo", [P, KH, NW], F32R)
        wo_f32 = sb("wo_f32", [P, KH, D])
        wo_scaled = sb("wo_scaled", [P, KH, D])
        wo_hi = sb("wo_hi", [P, KH, D], F32R)
        wo_lo = sb("wo_lo", [P, KH, D], F32R)
        nw_col = sb("nw_col", [P, KH])
        wg2_f32 = sb("wg2_f32", [P, D])
        wg2_hi = sb("wg2_hi", [P, D], F32R)
        wg2_stack = sb("wg2_stack", [P, D], F32R)
        w2_f32 = sb("w2_f32", [P, KH, D])
        w2_y = sb("w2_y", [P, KH, D])
        w2_m = sb("w2_m", [P, KH, D])
        w2_q = sb("w2_q", [P, KH, D], BF16)
        w2_nan = sb("w2_nan", [P, KH, D], BF16)
        w2_fp8 = sb("w2_fp8", [P, KH, D], BF16)
        scales = sb("scales", [P, 2])
        inv_scales = sb("inv_scales", [P, 2])
        descale = sb("descale", [P, 1])
        ld_row = sb("ld_row", [P, H])
        ld_col = sb("ld_col", [P, KH])
        ident = sb("ident", [P, P])
        ident_bf = sb("ident_bf", [P, P], BF16)
        ones_row = sb("ones_row", [P, P])
        lag = sb("lag", [P, P])
        lag_clamped = sb("lag_clamped", [P, P])
        decay_mask = sb("decay_mask", [P, 4, 4, 2, C])
        pos_row = sb("pos_row", [P, 2, C])
        q_decay = sb("q_decay", [P, KH, P])
        pos_col = sb("pos_col", [P, 1])
        pos_col64 = sb("pos_col64", [P, 1])
        k_logdecay = sb("k_logdecay", [P, H])
        k_decay = sb("k_decay", [P, H])
        chunk_decay = sb("chunk_decay", [P, KH])
        own_head = sb("own_head", [P, P])
        even_cols = sb("even_cols", [P, 4])
        head_parity = sb("head_parity", [P, 2])
        minus_half = sb("minus_half", [P, H])
        eps_col = sb("eps_col", [P, 1])

        bn6 = sb("bn6", [P, 2, 6])
        mean_var = sb("mean_var", [P, 2, 2])
        var_eps = sb("var_eps", [P, 2, 1])
        rstd = sb("rstd", [P, 2, 1])
        xn = sb("xn", [P, 2, D])
        e4_y = sb("e4_y", [P, D])
        e4_exp = sb("e4_exp", [P, D])
        e4_magic = sb("e4_magic", [P, D])
        e4_sum = sb("e4_sum", [P, D])
        e4_q = sb("e4_q", [P, D], BF16)
        e4_nan = sb("e4_nan", [P, D], BF16)
        xq = sb("xq", [P, 2, D], BF16)
        xT_hi = sb("xT_hi", [P, KH, P], F32R)
        xT_lo = sb("xT_lo", [P, KH, P], F32R)
        xqT = sb("xqT", [P, KH, P], BF16)
        kv = sb("kv", [P, 2, 2 * D])
        kd = sb("kd", [P, 2, D])
        q = sb("q", [P, D])
        g1_stack = sb("g1_stack", [P, P])
        g1T = sb("g1T", [P, P], F32R)
        kT = sb("kT", [P, 2, KH, P])
        qT = sb("qT", [P, 2, KH, 2, P])
        qdT = sb("qdT", [P, 2, KH, P])
        gate_tanh = sb("gate_tanh", [P, 2, D])
        ffn_silu = sb("ffn_silu", [P, 4, D])
        v_parity = sb("v_parity", [P, 2, 2, D])
        avT = sb("avT", [P, KH, P])
        probs = sb("probs", [P, 4, 4, 2 * C])
        state = sb("state", [P, KH, C])
        state_c0 = sb("state_c0", [P, 2, KH, P])
        state_c1 = sb("state_c1", [P, KH, P])
        og = sb("og", [P, D])
        og_sq = sb("og_sq", [P, D])
        og_sum = sb("og_sum", [P, H])
        og_var = sb("og_var", [P, H])
        og_rs = sb("og_rs", [P, H])
        og_y2 = sb("og_y2", [P, H])
        og_half = sb("og_half", [P, H])
        on = sb("on", [P, D])
        oT_hi = sb("oT_hi", [P, KH, P], F32R)
        oT_lo = sb("oT_lo", [P, KH, P], F32R)
        sg = sb("sg", [P, D])
        y = sb("y", [P, 2, D])

        def bank(name):
            return ctx.enter_context(nc.psum_tensor(name, [P, 512], F32))

        b_score = [bank("b_score0"), bank("b_score1")]
        b_kv = bank("b_kv")
        b_qg = bank("b_qg")
        b_xo = bank("b_xo")
        b_qk = bank("b_qk")
        b_gate = bank("b_gate")
        b_att = bank("b_att")
        ps_xT = b_xo[:, 0:D].rearrange("p (k t) -> p k t", k=KH)
        ps_oT = ps_xT
        ps_out = b_xo[:, D:2 * D]
        ps_xqT = b_gate[:, 0:P].bitcast(BF16).rearrange("p (k t) -> p k t", k=KH)
        ps_g1T = b_gate[:, 0:P]
        ps_gate = b_gate[:, 0:D]
        ps_ffn = b_gate[:, D:2 * D]
        ps_qT = b_qk[:, 0:D].rearrange("p (k t) -> p k t", k=KH)
        ps_kT = b_qk[:, D:2 * D].rearrange("p (k t) -> p k t", k=KH)
        ps_state = b_att[:, 0:KH * C].rearrange("p (k c) -> p k c", k=KH)
        ps_o = b_att[:, D:2 * D]
        ps_avT = b_score[0][:, D:2 * D].rearrange("p (k t) -> p k t", k=KH)

        s_x = sem("x_loaded")
        s_w = sem("w_loaded")
        s_w2 = sem("w2_loaded")
        s_small = sem("small_loaded")
        s_wo = sem("wo_loaded")
        s_pool = sem("pool_constants")
        s_dvec = sem("dve_constants")
        s_actc = sem("act_constants")
        s_whi = sem("w_hi_ready")
        s_wlo = sem("w_lo_ready")
        s_g2w = sem("wg2_loaded")
        s_g2 = sem("wg2_stack_ready")
        s_woready = sem("wo_parts_ready")
        s_w2q = sem("w2_quant_steps")
        s_bn = sem("bn_ready")
        s_mv = sem("mean_var_ready")
        s_ve = sem("var_eps_ready")
        s_rstd = sem("rstd_ready")
        s_xn = sem("xn_ready")
        s_y4 = sem("e4_y_ready")
        s_exp = sem("e4_exp_ready")
        s_e4 = sem("e4_magic_ready")
        s_nan = sem("e4_nan_ready")
        s_e4p = sem("e4_pool_steps")
        s_xq = sem("xq_ready")
        s_xTps = sem("xT_in_psum")
        s_xqTps = sem("xqT_in_psum")
        s_xThi = sem("xT_hi_ready")
        s_xTlo = sem("xT_lo_ready")
        s_xqT = sem("xqT_ready")
        s_kvps = sem("kv_in_psum")
        s_qgps = sem("qg_in_psum")
        s_kv = sem("kv_ready")
        s_q = sem("q_ready")
        s_kd = sem("kd_ready")
        s_g1hi = sem("g1_hi_ready")
        s_g1lo = sem("g1_lo_ready")
        s_g1Tps = sem("g1T_in_psum")
        s_g1T = sem("g1T_ready")
        s_ffnps = sem("ffn_in_psum")
        s_ffn = sem("ffn_silu_ready")
        s_gateps = sem("gate_in_psum")
        s_gate = sem("gate_tanh_ready")
        s_qkTps = sem("qkT_in_psum")
        s_qkT = sem("qkT_ready")
        s_qd = sem("qdT_ready")
        s_score = sem("scores_in_psum")
        s_probs = sem("probs_ready")
        s_kvs = sem("state_step_in_psum")
        s_state = sem("state_ready")
        s_sx = sem("state_masked_ready")
        s_vp = sem("v_parity_ready")
        s_avps = sem("avT_in_psum")
        s_av = sem("avT_ready")
        s_ops = sem("o_in_psum")
        s_og = sem("og_ready")
        s_sq = sem("og_sq_ready")
        s_sum = sem("og_sum_ready")
        s_rs = sem("og_rs_steps")
        s_on = sem("on_ready")
        s_oTps = sem("oT_in_psum")
        s_oThi = sem("oT_hi_ready")
        s_oTlo = sem("oT_lo_ready")
        s_outps = sem("out_in_psum")
        s_sg = sem("sg_ready")
        s_y = sem("y_ready")
        s_stored = sem("y_stored")

        x_v = x.rearrange("b (c p) d -> p (b c) d", p=P)
        out_v = out.rearrange("b (c p) d -> (b c) p d", p=P)

        def need(eng, s, v):
            if not isinstance(v, int) or v > 0:
                eng.wait_ge(s, v)

        def steps(program, prologue):
            def run(eng):
                prologue(eng)
                for j in range(2):
                    program(eng, 0, j)
                with eng.Fori(0, LOOPS) as i:
                    for j in range(2, NB + 2):
                        program(eng, i, j)
                for j in range(2, NB):
                    program(eng, LOOPS, j)
            return run

        def num(i, j):
            return NB * i + j

        def known(i, j):
            return not isinstance(i, int) or NB * i + j in range(G)

        def state_no(i, j, c):
            return (2 * NB - 1) * (i + j // NB) + 2 * (j % NB) + c

        block = ctx.enter_context(nc.Block())

        @block.sync
        def _(sp):
            def prologue(sp):
                lots = [(0, 1), (1, NB)] + [(NB * b, NB * b + NB) for b in range(1, B)]
                for n, (a, b) in enumerate(lots):
                    need(sp, s_x, 16 * n)
                    sp.dma_start(x_sb[:, a:b, :], x_v[:, a:b, :]).then_inc(s_x, 16)

            def store(sp, i, j):
                if not known(i, j - 2):
                    return
                sp.wait_ge(s_y, num(i, j - 1))
                dst = out_v[num(i, j - 2)] if isinstance(i, int) else out_v[bass.ds(num(i, j - 2), 1)].rearrange("a p d -> (a p) d")
                sp.dma_start(dst, y[:, (j - 2) % 2, :]).then_inc(s_stored, 16)

            steps(store, prologue)(sp)
            store(sp, LOOPS, NB)
            store(sp, LOOPS, NB + 1)
            sp.wait_ge(s_stored, 16 * G)

        @block.gpsimd
        def _(pool):
            g = nc.gpsimd

            def norm_factor(i, j):
                u = j % 2
                pool.wait_ge(s_mv, num(i, j) + 1)
                need(pool, s_xn, num(i, j) - 1)
                g.tensor_tensor(var_eps[:, u], mean_var[:, u, 1:2], eps_col[:], ALU.add).then_inc(s_ve, 1)
                pool.wait_ge(s_ve, num(i, j) + 1)
                g.tensor_tensor(rstd[:, u], var_eps[:, u], minus_half[:, 0:1], ALU.pow).then_inc(s_rstd, 1)

            def round_y(i, j):
                base = 2 * num(i, j)
                pool.wait_ge(s_e4, num(i, j) + 1)
                g.tensor_tensor(e4_sum[:], e4_y[:], e4_magic[:], ALU.add).then_inc(s_e4p, 1)
                pool.wait_ge(s_e4p, base + 1)
                need(pool, s_xq, num(i, j))
                g.tensor_tensor(e4_q[:], e4_sum[:], e4_magic[:], ALU.subtract).then_inc(s_e4p, 1)

            def put_nan(i, j):
                pool.wait_ge(s_nan, num(i, j) + 1)
                need(pool, s_xqTps, num(i, j) - 1)
                g.tensor_tensor(xq[:, j % 2], e4_q[:], e4_nan[:], ALU.add).then_inc(s_xq, 1)

            def decay_k(i, j):
                u = j % 2
                pool.wait_ge(s_kv, num(i, j) + 1)
                need(pool, s_ops, num(i, j) - 1)
                g.tensor_tensor(kd[:, u].rearrange("p (h e) -> p h e", h=H),
                                kv[:, u, 0:D].rearrange("p (h e) -> p h e", h=H),
                                k_decay[:].unsqueeze(2).broadcast_to([P, H, E]), ALU.mult).then_inc(s_kd, 1)

            def spread_state(i, j, c):
                if j % NB == NB - 1 and c == 1:
                    return
                made = state_no(i, j, c) + 1
                pool.wait_ge(s_state, 2 * made)
                dst = state_c1 if c == 0 else state_c0[:, (j + 1) % 2]
                need(pool, s_ops, num(i, j) if c == 0 else num(i, j) - 1)
                g.tensor_tensor(dst[:].rearrange("p k (b c) -> p k b c", b=2),
                                state[:].unsqueeze(2).broadcast_to([P, KH, 2, C]),
                                own_head[:].rearrange("p (b c) -> p b c", b=2).unsqueeze(1).broadcast_to([P, KH, 2, C]),
                                ALU.mult).then_inc(s_sx, 1)

            def head_norm(i, j):
                pool.wait_ge(s_rs, RS_STEPS * (num(i, j) + 1))
                need(pool, s_oTps, num(i, j))
                g.tensor_tensor(on[:].rearrange("p (h e) -> p h e", h=H), og[:].rearrange("p (h e) -> p h e", h=H),
                                og_rs[:].unsqueeze(2).broadcast_to([P, H, E]), ALU.mult).then_inc(s_on, 1)

            def add_x(i, j):
                pool.wait_ge(s_sg, num(i, j) + 1)
                need(pool, s_stored, 16 * num(i, j))
                xs = x_sb[:, num(i, j), :] if isinstance(i, int) else x_sb[:, bass.ds(num(i, j), 1), :].rearrange("p a d -> p (a d)")
                g.tensor_tensor(y[:, j % 2, :], sg[:], xs, ALU.add).then_inc(s_y, 1)

            def prologue(pool):
                g.memset(v_parity[:], 0.0)
                g.memset(minus_half[:], -0.5)
                g.memset(eps_col[:], EPS).then_inc(s_pool, 1)
                g.memset(ident[:], 0.0).then_inc(s_pool, 1)
                g.memset(ones_row[:], 1.0).then_inc(s_pool, 1)
                g.memset(wg2_f32[:], 0.0).then_inc(s_pool, 1)
                g.memset(g1_stack[:], 0.0).then_inc(s_pool, 1)
                g.memset(wg2_stack[:].bitcast(F32), 0.0).then_inc(s_pool, 1)
                pool.wait_ge(s_pool, 6)
                for r in range(4):
                    pool.dma_start(wg2_f32[32 * r:32 * r + GR, :], Wg2).then_inc(s_g2w, 16)
                g.affine_select(out=ident[:], in_=ident[:], compare_op=ALU.not_equal, fill=1.0, base=0,
                                pattern=[[-1, P]], channel_multiplier=1).then_inc(s_pool, 1)
                g.iota(lag[:], pattern=[[1, P]], base=0, channel_multiplier=-1, allow_small_or_imprecise_dtypes=True).then_inc(s_pool, 1)
                g.iota(pos_row[:], pattern=[[0, 2], [1, C]], base=1, channel_multiplier=0, allow_small_or_imprecise_dtypes=True).then_inc(s_pool, 1)
                g.iota(pos_col64[:], pattern=[[0, 1]], base=2 * C - 1, channel_multiplier=-1, allow_small_or_imprecise_dtypes=True).then_inc(s_pool, 1)
                pool.wait_ge(s_pool, 10)
                g.tensor_scalar(pos_col[0:C], pos_col64[0:C], -float(C), 1.0, ALU.add, ALU.mult).then_inc(s_pool, 1)
                pool.wait_ge(s_pool, 11)
                g.tensor_scalar(pos_col[C:P], pos_col64[C:P], 1.0, 0.0, ALU.mult, ALU.add).then_inc(s_pool, 1)
                pool.wait_ge(s_pool, 12)
                g.affine_select(out=own_head[:].rearrange("p (h e) -> p h e", h=HH), in_=ones_row[:].rearrange("p (h e) -> p h e", h=HH),
                                compare_op=ALU.is_ge, fill=0.0, base=0, pattern=[[-E, HH], [0, E]], channel_multiplier=1).then_inc(s_pool, 1)
                pool.wait_ge(s_pool, 13)
                g.affine_select(out=own_head[:].rearrange("p (h e) -> p h e", h=HH), in_=own_head[:].rearrange("p (h e) -> p h e", h=HH),
                                compare_op=ALU.is_ge, fill=0.0, base=E - 1, pattern=[[E, HH], [0, E]], channel_multiplier=-1).then_inc(s_pool, 1)
                g.affine_select(out=even_cols[:], in_=ones_row[:, 0:4], compare_op=ALU.is_ge, fill=0.0, base=0,
                                pattern=[[-2 * E, 4]], channel_multiplier=1).then_inc(s_pool, 1)
                pool.wait_ge(s_pool, 15)
                g.affine_select(out=even_cols[:], in_=even_cols[:], compare_op=ALU.is_ge, fill=0.0, base=E - 1,
                                pattern=[[2 * E, 4]], channel_multiplier=-1).then_inc(s_pool, 1)
                norm_factor(0, 0)
                norm_factor(0, 1)
                round_y(0, 0)
                put_nan(0, 0)
                pool.wait_ge(s_actc, H)
                dm = decay_mask[:].rearrange("p r i b c -> p (r i) (b c)")
                g.affine_select(out=dm, in_=dm, compare_op=ALU.is_ge, fill=0.0, base=0,
                                pattern=[[0, H], [1, P]], channel_multiplier=-1).then_inc(s_pool, 1)
                pool.wait_ge(s_pool, 17)
                g.memset(dm[0:C, :, C:P], 0.0).then_inc(s_pool, 1)
                pool.wait_ge(s_actc, H + 4)
                decay_k(0, 0)

            def step(pool, i, j):
                nxt, back, norm = known(i, j + 1), known(i, j - 1), known(i, j + 2)
                if nxt:
                    round_y(i, j + 1)
                    put_nan(i, j + 1)
                spread_state(i, j, 0)
                if norm:
                    norm_factor(i, j + 2)
                if nxt:
                    decay_k(i, j + 1)
                if known(i, j - 2):
                    add_x(i, j - 2)
                spread_state(i, j, 1)
                if back:
                    head_norm(i, j - 1)

            steps(step, prologue)(pool)
            add_x(LOOPS, NB - 2)
            head_norm(LOOPS, NB - 1)
            add_x(LOOPS, NB - 1)

        @block.scalar
        def _(act):
            a = nc.scalar

            def high_xT(i, j):
                act.wait_ge(s_xTps, num(i, j) + 1)
                need(act, s_qgps, num(i, j))
                a.activation(xT_hi[:], ps_xT, ACT.Copy).then_inc(s_xThi, 1)

            def copy_xqT(i, j):
                act.wait_ge(s_xqTps, num(i, j) + 1)
                need(act, s_ffnps, num(i, j))
                a.activation(xqT[:], ps_xqT, ACT.Copy).then_inc(s_xqT, 1)

            def silu_kv(i, j):
                act.wait_ge(s_kvps, num(i, j) + 1)
                need(act, s_ops, num(i, j) - 1)
                need(act, s_kd, num(i, j) - 1)
                a.activation(kv[:, j % 2], b_kv[:], ACT.Silu).then_inc(s_kv, 1)

            def silu_q(i, j):
                act.wait_ge(s_qgps, num(i, j) + 1)
                need(act, s_qkTps, num(i, j))
                a.activation(q[:], b_qg[:, 0:D], ACT.Silu).then_inc(s_q, 1)
                need(act, s_g1Tps, num(i, j))
                a.activation(g1_stack[:, 0:64].bitcast(F32R).rearrange("p (r c) -> p r c", r=2)[:, :, 0:GR],
                             b_qg[:, D:D + GR].unsqueeze(1).broadcast_to([P, 2, GR]), ACT.Copy).then_inc(s_g1hi, 1)

            def silu_ffn(i, j):
                act.wait_ge(s_ffnps, num(i, j) + 1)
                need(act, s_sg, num(i, j) - 2)
                a.activation(ffn_silu[:, j % 4], ps_ffn, ACT.Silu, scale=descale[:, 0:1]).then_inc(s_ffn, 1)

            def copy_g1T(i, j):
                act.wait_ge(s_g1Tps, num(i, j) + 1)
                need(act, s_gateps, num(i, j))
                a.activation(g1T[:], ps_g1T, ACT.Copy).then_inc(s_g1T, 1)

            def copy_kT(i, j):
                u = j % 2
                act.wait_ge(s_qkTps, num(i, j) + 1)
                need(act, s_score, 4 * (num(i, j) - 1))
                a.activation(kT[:, u], ps_kT, ACT.Copy).then_inc(s_qkT, 1)

            def copy_qT(i, j):
                u = j % 2
                for par in range(2):
                    a.activation(qT[:, u, :, par, :], ps_qT, ACT.Copy, scale=head_parity[:, par:par + 1]).then_inc(s_qkT, 1)

            def gate(i, j):
                act.wait_ge(s_gateps, num(i, j) + 1)
                need(act, s_og, num(i, j) - 1)
                a.activation(gate_tanh[:, j % 2], ps_gate, ACT.Tanh, scale=0.5).then_inc(s_gate, 1)

            def high_oT(i, j):
                act.wait_ge(s_oTps, num(i, j) + 1)
                need(act, s_outps, num(i, j))
                a.activation(oT_hi[:], ps_oT, ACT.Copy).then_inc(s_oThi, 1)

            def scale_y(i, j):
                act.wait_ge(s_xn, num(i, j) + 1)
                need(act, s_e4p, 2 * num(i, j))
                a.activation(e4_y[:], xn[:, j % 2], ACT.Copy, scale=scales[:, 0:1]).then_inc(s_y4, 1)

            def square_o(i, j):
                act.wait_ge(s_og, num(i, j) + 1)
                need(act, s_sum, num(i, j))
                a.activation(og_sq[:], og[:], ACT.Square).then_inc(s_sq, 1)

            def copy_avT(i, j):
                act.wait_ge(s_avps, num(i, j) + 1)
                need(act, s_ops, num(i, j))
                a.activation(avT[:], ps_avT, ACT.Copy).then_inc(s_av, 1)

            def prologue(act):
                for kk in range(KH):
                    act.dma_start(w_f32[:, kk, 0:D], Wk[kk * P:kk * P + P, :]).then_inc(s_w, 16)
                    act.dma_start(w_f32[:, kk, D:2 * D], Wv[kk * P:kk * P + P, :]).then_inc(s_w, 16)
                    act.dma_start(w_f32[:, kk, Q0:Q0 + D], Wq[kk * P:kk * P + P, :]).then_inc(s_w, 16)
                    act.dma_start(w_f32[:, kk, 3 * D:NW], Wg1[kk * P:kk * P + P, :]).then_inc(s_w, 16)
                act.dma_start(ld_row[:], log_decay.unsqueeze(0).broadcast_to([P, H])).then_inc(s_small, 16)
                for half in range(KH):
                    act.dma_start(ld_col[:, half:half + 1],
                                  log_decay[half * HH:half * HH + HH].unsqueeze(1).broadcast_to([HH, E])).then_inc(s_small, 16)
                act.dma_start(scales[:, 0:1], scale.unsqueeze(0).broadcast_to([P, 1])).then_inc(s_small, 16)
                act.dma_start(scales[:, 1:2], scale1.unsqueeze(0).broadcast_to([P, 1])).then_inc(s_small, 16)
                act.dma_start(w2_f32[:], W2.rearrange("(k p) n -> p k n", p=P)).then_inc(s_w2, 16)
                act.dma_start(wo_f32[:], Wo.rearrange("(k p) n -> p k n", p=P)).then_inc(s_wo, 16)
                for kk in range(KH):
                    act.dma_start(nw_col[:, kk:kk + 1], norm_w[kk * P:kk * P + P].unsqueeze(1)).then_inc(s_wo, 16)
                act.wait_ge(s_small, 80)
                act.wait_ge(s_dvec, 1)
                for r in range(4):
                    for k in range(4):
                        h = HH * (k // 2) + 2 * r + k % 2
                        a.activation(decay_mask[:, r, k].rearrange("p b c -> p (b c)"), lag_clamped[:], ACT.Exp,
                                     scale=ld_row[:, h:h + 1]).then_inc(s_actc, 1)
                for half in range(KH):
                    a.activation(q_decay[:, half], pos_row[:].rearrange("p b c -> p (b c)"), ACT.Exp,
                                 scale=ld_col[:, half:half + 1]).then_inc(s_actc, 1)
                act.wait_ge(s_dvec, 2)
                a.activation(k_decay[:], k_logdecay[:], ACT.Exp).then_inc(s_actc, 1)
                a.activation(chunk_decay[:], ld_col[:], ACT.Exp, scale=float(C)).then_inc(s_actc, 1)
                act.wait_ge(s_w, 128)
                for kk in range(KH):
                    a.activation(w_hi[:, kk], w_f32[:, kk], ACT.Copy).then_inc(s_whi, 1)
                act.wait_ge(s_dvec, 6)
                scale_y(0, 0)
                high_xT(0, 0)
                copy_xqT(0, 0)
                silu_kv(0, 0)
                silu_q(0, 0)
                scale_y(0, 1)
                silu_ffn(0, 0)
                copy_g1T(0, 0)
                copy_kT(0, 0)
                copy_qT(0, 0)
                gate(0, 0)

            def step(act, i, j):
                nxt, back, norm = known(i, j + 1), known(i, j - 1), known(i, j + 2)
                if back:
                    square_o(i, j - 1)
                if nxt:
                    high_xT(i, j + 1)
                    silu_kv(i, j + 1)
                    silu_q(i, j + 1)
                    copy_xqT(i, j + 1)
                copy_avT(i, j)
                if nxt:
                    silu_ffn(i, j + 1)
                    copy_kT(i, j + 1)
                if back:
                    high_oT(i, j - 1)
                if nxt:
                    copy_qT(i, j + 1)
                    copy_g1T(i, j + 1)
                if norm:
                    scale_y(i, j + 2)
                if nxt:
                    gate(i, j + 1)

            steps(step, prologue)(act)
            square_o(LOOPS, NB - 1)
            high_oT(LOOPS, NB - 1)

        @block.vector
        def _(dve):
            v = nc.vector

            def stats(i, j):
                u = j % 2
                if isinstance(i, int) and NB * i + j == 0:
                    dve.wait_ge(s_x, 16)
                else:
                    dve.wait_ge(s_x, 16 * (i + j // NB) + 32)
                xs = x_sb[:, num(i, j), :] if isinstance(i, int) else x_sb[:, bass.ds(num(i, j), 1), :].rearrange("p a d -> p (a d)")
                v.bn_stats(bn6[:, u], xs).then_inc(s_bn, 1)

            def aggregate_waits(i, j):
                dve.wait_ge(s_bn, num(i, j) + 1)
                need(dve, s_ve, num(i, j) - 1)

            def aggregate(i, j):
                u = j % 2
                v.bn_aggr(mean_var[:, u], bn6[:, u]).then_inc(s_mv, 1)

            def normalise(i, j):
                u = j % 2
                dve.wait_ge(s_mv, num(i, j) + 1)
                dve.wait_ge(s_rstd, num(i, j) + 1)
                need(dve, s_xTps, num(i, j) - 1)
                need(dve, s_y4, num(i, j) - 1)
                xs = x_sb[:, num(i, j), :] if isinstance(i, int) else x_sb[:, bass.ds(num(i, j), 1), :].rearrange("p a d -> p (a d)")
                v.tensor_scalar(xn[:, u], xs, mean_var[:, u, 0:1], rstd[:, u, 0:1], ALU.subtract, ALU.mult).then_inc(s_xn, 1)

            def exponent(i, j):
                dve.wait_ge(s_y4, num(i, j) + 1)
                need(dve, s_e4p, 2 * num(i, j))
                v.tensor_scalar(e4_exp[:].bitcast(I32), e4_y[:].bitcast(I32), 0x7F800000, None, ALU.bitwise_and).then_inc(s_exp, 1)

            def magic(i, j):
                dve.wait_ge(s_exp, num(i, j) + 1)
                v.tensor_scalar(e4_magic[:], e4_exp[:], E4_MIN, E4_MAGIC, ALU.max, ALU.mult).then_inc(s_e4, 1)

            def find_nan(i, j):
                dve.wait_ge(s_e4p, 2 * (num(i, j) + 1))
                need(dve, s_xq, num(i, j))
                v.tensor_scalar(e4_nan[:], e4_q[:], E4_OVER, 0.0, ALU.mult, ALU.mult).then_inc(s_nan, 1)

            def low_xT(i, j):
                dve.wait_ge(s_xThi, num(i, j) + 1)
                need(dve, s_qgps, num(i, j))
                v.tensor_tensor(xT_lo[:], ps_xT, xT_hi[:].bitcast(F32), ALU.subtract).then_inc(s_xTlo, 1)

            def low_g1(i, j):
                dve.wait_ge(s_g1hi, num(i, j) + 1)
                v.tensor_tensor(g1_stack[:, 64:128].bitcast(F32R).rearrange("p (r c) -> p r c", r=2)[:, :, 0:GR],
                                b_qg[:, D:D + GR].unsqueeze(1).broadcast_to([P, 2, GR]),
                                g1_stack[:, 0:64].rearrange("p (r c) -> p r c", r=2)[:, :, 0:GR],
                                ALU.subtract).then_inc(s_g1lo, 1)

            def mask(i, j, r):
                dve.wait_ge(s_score, 4 * num(i, j) + r + 1)
                need(dve, s_ops, num(i, j))
                v.tensor_tensor(probs[:, r].rearrange("p i (b c) -> p i b c", b=2),
                                b_score[r % 2][:, 0:4 * C].rearrange("p (i c) -> p i c", i=4).unsqueeze(2).broadcast_to([P, 4, 2, C]),
                                decay_mask[:, r], ALU.mult).then_inc(s_probs, 1)

            def add_state(i, j, c):
                if j % NB == NB - 1 and c == 1:
                    return
                dve.wait_ge(s_kvs, state_no(i, j, c) + 1)
                if j % NB == 0 and c == 0:
                    need(dve, s_sx, state_no(i, j, c))
                    v.tensor_copy(state[:], ps_state).then_inc(s_state, 2)
                else:
                    dve.wait_ge(s_state, 2 * state_no(i, j, c))
                    dve.wait_ge(s_sx, state_no(i, j, c))
                    for half in range(KH):
                        v.scalar_tensor_tensor(out=state[:, half], in0=state[:, half], scalar=chunk_decay[:, half:half + 1],
                                               in1=ps_state[:, half], op0=ALU.mult, op1=ALU.add).then_inc(s_state, 1)

            def decay_q(i, j):
                dve.wait_ge(s_qkT, 3 * (num(i, j) + 1))
                need(dve, s_ops, num(i, j) - 1)
                v.tensor_tensor(qdT[:, j % 2], ps_qT, q_decay[:], ALU.mult).then_inc(s_qd, 1)

            def gate_o(i, j):
                dve.wait_ge(s_ops, num(i, j) + 1)
                dve.wait_ge(s_gate, num(i, j) + 1)
                need(dve, s_on, num(i, j))
                v.scalar_tensor_tensor(out=og[:], in0=gate_tanh[:, j % 2], scalar=1.0, in1=ps_o,
                                       op0=ALU.add, op1=ALU.mult).then_inc(s_og, 1)

            def sum_heads(i, j):
                dve.wait_ge(s_sq, num(i, j) + 1)
                need(dve, s_rs, RS_STEPS * num(i, j))
                v.tensor_reduce(og_sum[:], og_sq[:].rearrange("p (h e) -> p h e", h=H), AX_X, ALU.add).then_inc(s_sum, 1)

            def rsqrt(i, j, first, last):
                for m in range(first, last):
                    if m == 0:
                        dve.wait_ge(s_sum, num(i, j) + 1)
                        need(dve, s_on, num(i, j))
                    else:
                        dve.wait_ge(s_rs, RS_STEPS * num(i, j) + m)
                    if m == 0:
                        ins = v.tensor_scalar(og_var[:], og_sum[:], 1.0 / E, 4.0 * EPS, ALU.mult, ALU.add)
                    elif m == 1:
                        ins = v.tensor_scalar(og_half[:].bitcast(I32), og_var[:].bitcast(I32), 1, None, ALU.logical_shift_right)
                    elif m == 2:
                        ins = v.tensor_scalar(og_rs[:].bitcast(I32), og_half[:].bitcast(I32), -1.0, float(0x5F3759DF), ALU.mult, ALU.add)
                    elif m % 3 == 0:
                        ins = v.tensor_tensor(og_y2[:], og_rs[:], og_rs[:], ALU.mult)
                    elif m % 3 == 1:
                        ins = v.scalar_tensor_tensor(out=og_half[:], in0=og_y2[:], scalar=-0.5, in1=og_var[:], op0=ALU.mult, op1=ALU.mult)
                    else:
                        ins = v.scalar_tensor_tensor(out=og_rs[:], in0=og_half[:], scalar=1.5, in1=og_rs[:], op0=ALU.add, op1=ALU.mult)
                    ins.then_inc(s_rs, 1)

            def part_v(i, j):
                u = j % 2
                dve.wait_ge(s_kv, num(i, j) + 1)
                need(dve, s_avps, num(i, j) - 1)
                src = kv[:, u, D:2 * D].rearrange("p (a b e) -> p a b e", a=HH, b=2)
                for par in range(2):
                    dst = v_parity[:, u, par].rearrange("p (a b e) -> p a b e", a=HH, b=2)
                    v.tensor_copy(dst[:, :, par], src[:, :, par]).then_inc(s_vp, 1)

            def low_oT(i, j):
                dve.wait_ge(s_oThi, num(i, j) + 1)
                need(dve, s_outps, num(i, j))
                v.tensor_tensor(oT_lo[:], ps_oT, oT_hi[:].bitcast(F32), ALU.subtract).then_inc(s_oTlo, 1)

            def product(i, j):
                dve.wait_ge(s_outps, num(i, j) + 1)
                dve.wait_ge(s_ffn, num(i, j) + 1)
                need(dve, s_y, num(i, j))
                v.tensor_tensor(sg[:], ps_out, ffn_silu[:, j % 4], ALU.mult).then_inc(s_sg, 1)

            def prologue(dve):
                stats(0, 0)
                aggregate_waits(0, 0)
                aggregate(0, 0)
                dve.wait_ge(s_pool, 12)
                v.tensor_scalar(lag_clamped[:], lag[:], 0.0, None, ALU.max).then_inc(s_dvec, 1)
                normalise(0, 0)
                stats(0, 1)
                aggregate_waits(0, 1)
                aggregate(0, 1)
                dve.wait_ge(s_small, 80)
                v.tensor_scalar(k_logdecay[:], ld_row[:], pos_col[:, 0:1], None, ALU.mult).then_inc(s_dvec, 1)
                v.tensor_copy(ident_bf[:], ident[:]).then_inc(s_dvec, 1)
                v.reciprocal(inv_scales[:], scales[:]).then_inc(s_dvec, 1)
                dve.wait_ge(s_dvec, 4)
                v.tensor_scalar(descale[:], inv_scales[:, 0:1], inv_scales[:, 1:2], None, ALU.mult).then_inc(s_dvec, 1)
                dve.wait_ge(s_pool, 16)
                v.tensor_reduce(head_parity[:, 0:1], even_cols[:], AX_X, ALU.add).then_inc(s_dvec, 1)
                dve.wait_ge(s_dvec, 6)
                v.tensor_scalar(head_parity[:, 1:2], head_parity[:, 0:1], -1.0, 1.0, ALU.mult, ALU.add).then_inc(s_dvec, 1)
                exponent(0, 0)
                magic(0, 0)
                normalise(0, 1)
                find_nan(0, 0)
                for kk in range(KH):
                    dve.wait_ge(s_whi, kk + 1)
                    v.tensor_tensor(w_lo[:, kk], w_f32[:, kk], w_hi[:, kk].bitcast(F32), ALU.subtract).then_inc(s_wlo, 1)
                low_xT(0, 0)
                dve.wait_ge(s_w2, 16)
                v.tensor_scalar(w2_y[:], w2_f32[:], scales[:, 1:2], None, ALU.mult).then_inc(s_w2q, 1)
                dve.wait_ge(s_w2q, 1)
                v.tensor_scalar(w2_m[:].bitcast(I32), w2_y[:].bitcast(I32), 0x7F800000, None, ALU.bitwise_and).then_inc(s_w2q, 1)
                dve.wait_ge(s_w2q, 2)
                v.tensor_scalar(w2_f32[:], w2_m[:], E4_MIN, E4_MAGIC, ALU.max, ALU.mult).then_inc(s_w2q, 1)
                dve.wait_ge(s_w2q, 3)
                v.tensor_tensor(w2_m[:], w2_y[:], w2_f32[:], ALU.add).then_inc(s_w2q, 1)
                dve.wait_ge(s_w2q, 4)
                v.tensor_tensor(w2_q[:], w2_m[:], w2_f32[:], ALU.subtract).then_inc(s_w2q, 1)
                dve.wait_ge(s_w2q, 5)
                v.tensor_scalar(w2_nan[:], w2_q[:], E4_OVER, 0.0, ALU.mult, ALU.mult).then_inc(s_w2q, 1)
                dve.wait_ge(s_w2q, 6)
                v.tensor_tensor(w2_fp8[:], w2_q[:], w2_nan[:], ALU.add).then_inc(s_w2q, 1)
                low_g1(0, 0)
                dve.wait_ge(s_g2w, 64)
                dve.wait_ge(s_pool, 6)
                v.tensor_copy(wg2_hi[:], wg2_f32[:]).then_inc(s_g2, 1)
                dve.wait_ge(s_g2, 1)
                for r in range(4):
                    rows = slice(32 * r, 32 * r + GR)
                    if r % 2 == 0:
                        v.tensor_copy(wg2_stack[rows], wg2_f32[rows]).then_inc(s_g2, 1)
                    else:
                        v.tensor_tensor(wg2_stack[rows], wg2_f32[rows], wg2_hi[rows].bitcast(F32), ALU.subtract).then_inc(s_g2, 1)
                dve.wait_ge(s_pool, 1)
                part_v(0, 0)
                dve.wait_ge(s_actc, H + 4)
                decay_q(0, 0)
                dve.wait_ge(s_wo, 48)
                for kk in range(KH):
                    v.tensor_scalar(wo_scaled[:, kk], wo_f32[:, kk], nw_col[:, kk:kk + 1], None, ALU.mult).then_inc(s_woready, 1)
                dve.wait_ge(s_woready, 2)
                v.tensor_copy(wo_hi[:], wo_scaled[:]).then_inc(s_woready, 1)
                dve.wait_ge(s_woready, 3)
                v.tensor_tensor(wo_lo[:], wo_scaled[:], wo_hi[:].bitcast(F32), ALU.subtract).then_inc(s_woready, 1)
                dve.wait_ge(s_pool, 18)

            def step(dve, i, j):
                nxt, back, norm = known(i, j + 1), known(i, j - 1), known(i, j + 2)

                def newton(first, last):
                    if back:
                        rsqrt(i, j - 1, first, last)

                if back:
                    gate_o(i, j - 1)
                if nxt:
                    exponent(i, j + 1)
                mask(i, j, 0)
                if nxt:
                    magic(i, j + 1)
                    low_xT(i, j + 1)
                if back:
                    sum_heads(i, j - 1)
                mask(i, j, 1)
                newton(0, 1)
                add_state(i, j, 0)
                newton(1, 2)
                if nxt:
                    find_nan(i, j + 1)
                newton(2, 3)
                if norm:
                    stats(i, j + 2)
                newton(3, 4)
                if norm:
                    aggregate_waits(i, j + 2)
                newton(4, 5)
                if norm:
                    aggregate(i, j + 2)
                newton(5, 6)
                mask(i, j, 2)
                newton(6, 7)
                if nxt:
                    part_v(i, j + 1)
                newton(7, 8)
                add_state(i, j, 1)
                newton(8, 9)
                if nxt:
                    low_g1(i, j + 1)
                newton(9, 10)
                mask(i, j, 3)
                newton(10, 11)
                if norm:
                    normalise(i, j + 2)
                newton(11, 12)
                if back:
                    low_oT(i, j - 1)
                if nxt:
                    decay_q(i, j + 1)
                if back:
                    product(i, j - 1)

            steps(step, prologue)(dve)
            gate_o(LOOPS, NB - 1)
            sum_heads(LOOPS, NB - 1)
            rsqrt(LOOPS, NB - 1, 0, RS_STEPS)
            low_oT(LOOPS, NB - 1)
            product(LOOPS, NB - 1)

        @block.tensor
        def _(pe):
            t = nc.tensor

            def transpose_x(i, j):
                u = j % 2
                pe.wait_ge(s_xn, num(i, j) + 1)
                need(pe, s_sg, num(i, j) - 2)
                for kk in range(KH):
                    mm = t.transpose(ps_xT[:, kk, :], xn[:, u, kk * P:kk * P + P], ident[:])
                mm.then_inc(s_xTps, 1)

            def transpose_xq(i, j):
                u = j % 2
                pe.wait_ge(s_xq, num(i, j) + 1)
                need(pe, s_gate, num(i, j))
                for kk in range(KH):
                    mm = t.transpose(ps_xqT[:, kk, :], xq[:, u, kk * P:kk * P + P], ident_bf[:])
                mm.then_inc(s_xqTps, 1)

            def project(i, j, dst, a, b, s_done, s_free, free):
                pe.wait_ge(s_xThi, num(i, j) + 1)
                need(pe, s_free, free)
                for kk in range(KH):
                    t.matmul(dst, xT_hi[:, kk], w_hi[:, kk, a:b], start=(kk == 0), stop=False)
                for kk in range(KH):
                    t.matmul(dst, xT_hi[:, kk], w_lo[:, kk, a:b], start=False, stop=False)
                pe.wait_ge(s_xTlo, num(i, j) + 1)
                for kk in range(KH):
                    mm = t.matmul(dst, xT_lo[:, kk], w_hi[:, kk, a:b], start=False, stop=(kk == KH - 1))
                mm.then_inc(s_done, 1)

            def project_kv(i, j):
                project(i, j, b_kv[:, :], 0, 2 * D, s_kvps, s_kv, num(i, j))

            def project_qg(i, j):
                project(i, j, b_qg[:, 0:NW - Q0], Q0, NW, s_qgps, s_g1lo, num(i, j))

            def ffn(i, j):
                pe.wait_ge(s_xqT, num(i, j) + 1)
                for kk in range(KH):
                    mm = t.matmul(ps_ffn, xqT[:, kk], w2_fp8[:, kk], start=(kk == 0), stop=(kk == KH - 1))
                mm.then_inc(s_ffnps, 1)

            def transpose_g1(i, j):
                pe.wait_ge(s_g1lo, num(i, j) + 1)
                pe.wait_ge(s_ffn, num(i, j) + 1)
                t.transpose(ps_g1T, g1_stack[:], ident[:]).then_inc(s_g1Tps, 1)

            def transpose_qk(i, j):
                pe.wait_ge(s_kv, num(i, j) + 1)
                pe.wait_ge(s_q, num(i, j) + 1)
                need(pe, s_qd, num(i, j))
                for kk in range(KH):
                    t.transpose(ps_qT[:, kk, :], q[:, kk * P:kk * P + P], ident[:])
                for kk in range(KH):
                    mm = t.transpose(ps_kT[:, kk, :], kv[:, j % 2, kk * P:kk * P + P], ident[:])
                mm.then_inc(s_qkTps, 1)

            def gate(i, j):
                pe.wait_ge(s_g1T, num(i, j) + 1)
                t.matmul(ps_gate, g1T[:], wg2_stack[:], start=True, stop=True).then_inc(s_gateps, 1)

            def scores(i, j, r):
                u = j % 2
                if r == 0:
                    pe.wait_ge(s_qkT, 3 * (num(i, j) + 1))
                    need(pe, s_av, num(i, j))
                need(pe, s_probs, 4 * num(i, j) + r - 1)
                rows = slice(32 * r, 32 * r + 32)
                for half in range(KH):
                    for c in range(2):
                        mm = t.matmul(b_score[r % 2][c * C:c * C + C, half * 2 * C:(half + 1) * 2 * C],
                                      kT[rows, u, half, c * C:c * C + C], qT[rows, u, half, :, c * C:c * C + C],
                                      start=True, stop=True)
                mm.then_inc(s_score, 1)

            def state_waits(i, j, c):
                if c == 0:
                    pe.wait_ge(s_kd, num(i, j) + 1)
                    need(pe, s_og, num(i, j))
                else:
                    pe.wait_ge(s_state, 2 * state_no(i, j, 1))

            def state_step(i, j, c):
                if j % NB == NB - 1 and c == 1:
                    return
                u = j % 2
                rows = slice(c * C, c * C + C)
                for half in range(KH):
                    for b in range(2):
                        cols = slice(half * P + b * C, half * P + b * C + C)
                        mm = t.matmul(ps_state[b * C:b * C + C, half, :], kd[rows, u, cols],
                                      kv[rows, u, D + cols.start:D + cols.stop], start=True, stop=True)
                mm.then_inc(s_kvs, 1)

            def from_chunk(i, j):
                u = j % 2
                pe.wait_ge(s_probs, 4 * (num(i, j) + 1))
                pe.wait_ge(s_vp, 2 * (num(i, j) + 1))
                for half in range(KH):
                    for par in range(2):
                        for r in range(4):
                            mm = t.matmul(ps_avT[32 * r:32 * r + 32, half, :],
                                          v_parity[:, u, par, half * P + 32 * r:half * P + 32 * r + 32],
                                          probs[:, r, 2 * half + par, :], start=(par == 0), stop=(par == 1),
                                          skip_group_check=True)
                mm.then_inc(s_avps, 1)

            def from_state(i, j):
                u = j % 2
                pe.wait_ge(s_qd, num(i, j) + 1)
                pe.wait_ge(s_sx, state_no(i, j, 1))
                if j % NB == NB - 1:
                    pe.wait_ge(s_state, 2 * state_no(i, j, 1))
                else:
                    pe.wait_ge(s_state, 2 * state_no(i, j, 1) + 2)
                for c in range(1 if j % NB == 0 else 0, 2):
                    st = state_c0[:, u] if c == 0 else state_c1
                    for half in range(KH):
                        t.matmul(ps_o[c * C:c * C + C, half * P:half * P + P], qdT[:, u, half, c * C:c * C + C],
                                 st[:, half, :], start=(half == 0), stop=False, skip_group_check=True)

            def add_chunk(i, j):
                first = j % NB == 0
                pe.wait_ge(s_av, num(i, j) + 1)
                if first:
                    for half in range(KH):
                        t.matmul(ps_o[0:C, half * P:half * P + P], avT[:, half, 0:C], ident[:],
                                 start=(half == 0), stop=True, skip_group_check=True)
                    for half in range(KH):
                        mm = t.matmul(ps_o[C:P, half * P:half * P + P], avT[:, half, C:P], ident[:],
                                      start=False, stop=True, skip_group_check=True)
                else:
                    for half in range(KH):
                        mm = t.matmul(ps_o[:, half * P:half * P + P], avT[:, half, :], ident[:],
                                      start=False, stop=True, skip_group_check=True)
                mm.then_inc(s_ops, 1)

            def transpose_o(i, j):
                pe.wait_ge(s_on, num(i, j) + 1)
                if known(i, j + 2):
                    pe.wait_ge(s_xTlo, num(i, j) + 3)
                for kk in range(KH):
                    mm = t.transpose(ps_oT[:, kk, :], on[:, kk * P:kk * P + P], ident[:])
                mm.then_inc(s_oTps, 1)

            def project_o(i, j):
                pe.wait_ge(s_oTlo, num(i, j) + 1)
                parts = [(oT_hi, wo_hi), (oT_hi, wo_lo), (oT_lo, wo_hi)]
                for n, (lhs, rhs) in enumerate(parts):
                    for kk in range(KH):
                        mm = t.matmul(ps_out, lhs[:, kk], rhs[:, kk], start=(n == 0 and kk == 0), stop=(n == 2 and kk == KH - 1))
                mm.then_inc(s_outps, 1)

            def prologue(pe):
                pe.wait_ge(s_pool, 7)
                pe.wait_ge(s_dvec, 3)
                transpose_x(0, 0)
                pe.wait_ge(s_wlo, 2)
                project_kv(0, 0)
                transpose_xq(0, 0)
                project_qg(0, 0)
                pe.wait_ge(s_w2q, 7)
                ffn(0, 0)
                transpose_g1(0, 0)
                transpose_qk(0, 0)
                pe.wait_ge(s_g2, 5)
                gate(0, 0)
                pe.wait_ge(s_woready, 4)

            def step(pe, i, j):
                nxt, back = known(i, j + 1), known(i, j - 1)
                scores(i, j, 0)
                if nxt:
                    transpose_x(i, j + 1)
                state_waits(i, j, 0)
                scores(i, j, 1)
                state_step(i, j, 0)
                if nxt:
                    project_kv(i, j + 1)
                state_waits(i, j, 1)
                scores(i, j, 2)
                state_step(i, j, 1)
                if nxt:
                    project_qg(i, j + 1)
                scores(i, j, 3)
                if nxt:
                    transpose_xq(i, j + 1)
                from_chunk(i, j)
                if nxt:
                    ffn(i, j + 1)
                    transpose_qk(i, j + 1)
                if back:
                    transpose_o(i, j - 1)
                from_state(i, j)
                if nxt:
                    transpose_g1(i, j + 1)
                add_chunk(i, j)
                if back:
                    project_o(i, j - 1)
                if nxt:
                    gate(i, j + 1)

            steps(step, prologue)(pe)
            transpose_o(LOOPS, NB - 1)
            project_o(LOOPS, NB - 1)


_INS = ['L0_attn_x', 'L0_attn_log_decay', 'L0_attn_Wq', 'L0_attn_Wk', 'L0_attn_Wv', 'L0_attn_Wo', 'L0_attn_Wg1',
        'L0_attn_Wg2', 'L0_attn_norm_w', 'L0_ffn_input2', 'L0_ffn_scale', 'L0_ffn_scale1']
_OUTS = [((4, 512, 256), 'float32')]


def kernel(**inputs):
    import numpy as _np
    import concourse.bacc as _bacc
    from concourse import mybir as _mybir
    from concourse.bass_utils import run_bass_kernel_spmd as _run

    nc = _bacc.Bacc("TRN2", target_bir_lowering=False, num_devices=1)
    arrays, args = {}, []
    for name in _INS:
        a = _np.ascontiguousarray(inputs[name])
        if a.ndim == 0:
            a = a.reshape(1)
        arrays[f"in_{name}_dram"] = a
        args.append(nc.dram_tensor(f"in_{name}_dram", a.shape, _mybir.dt.from_np(a.dtype), kind="ExternalInput").ap())
    for i, (shape, dtype) in enumerate(_OUTS):
        dt = _mybir.dt.from_np(_np.dtype(dtype))
        args.append(nc.dram_tensor(f"out_{i}_dram", shape, dt, kind="ExternalOutput").ap())
    layer_kernel(nc, *args)
    r = _run(nc, [arrays], core_ids=[0])
    return r.results[0]["out_0_dram"]
```

```python
from contextlib import ExitStack

import concourse.bass as bass
from concourse import mybir

F32 = mybir.dt.float32
F32R = mybir.dt.float32r
BF16 = mybir.dt.bfloat16
I32 = mybir.dt.int32
ALU = mybir.AluOpType
ACT = mybir.ActivationFunctionType
AX_X = mybir.AxisListType.X

P = 128
EPS = 1e-5


def layer_kernel(nc, x, log_decay, Wq, Wk, Wv, Wo, Wg1, Wg2, norm_w, W2, scale, scale1, out):
    B, N, D = x.shape
    H = log_decay.shape[0]
    E = D // H
    NB = N // P
    G = B * NB
    KH = D // P
    HH = H // KH
    C = P // 2
    GR = Wg1.shape[1]
    Q0 = 2 * D
    NW = 3 * D + GR
    LOOPS = B - 1
    RS_STEPS = 12
    WO_LOADS = 16 * (1 + KH)
    assert (P, NB, KH, HH, E, GR) == (128, 4, 2, 8, 16, 16)

    E4_MIN = 2.0 ** -6
    E4_MAGIC = 1.5 * 2.0 ** 20
    E4_OVER = (2.0 ** 127) / 232.0

    with ExitStack() as ctx:
        def sb(name, shape, dt=F32):
            return ctx.enter_context(nc.sbuf_tensor(name, shape, dt))

        def sem(name):
            return ctx.enter_context(nc.semaphore(name))

        x_sb = sb("x_sb", [P, G, D])
        w_f32 = sb("w_f32", [P, KH, NW])
        w_hi = sb("w_hi", [P, KH, NW], F32R)
        w_lo = sb("w_lo", [P, KH, NW], F32R)
        wo_f32 = sb("wo_f32", [P, KH, D])
        wo_scaled = sb("wo_scaled", [P, KH, D])
        wo_hi = sb("wo_hi", [P, KH, D], F32R)
        wo_lo = sb("wo_lo", [P, KH, D], F32R)
        nw_col = sb("nw_col", [P, KH])
        wg2_f32 = sb("wg2_f32", [P, D])
        wg2_hi = sb("wg2_hi", [P, D], F32R)
        wg2_stack = sb("wg2_stack", [P, D], F32R)
        w2_f32 = sb("w2_f32", [P, KH, D])
        w2_y = sb("w2_y", [P, KH, D])
        w2_m = sb("w2_m", [P, KH, D])
        w2_q = sb("w2_q", [P, KH, D], BF16)
        w2_nan = sb("w2_nan", [P, KH, D], BF16)
        w2_fp8 = sb("w2_fp8", [P, KH, D], BF16)
        scales = sb("scales", [P, 2])
        inv_scales = sb("inv_scales", [P, 2])
        descale = sb("descale", [P, 1])
        ld_row = sb("ld_row", [P, H])
        ld_col = sb("ld_col", [P, KH])
        ident = sb("ident", [P, P])
        ident_bf = sb("ident_bf", [P, P], BF16)
        ones_row = sb("ones_row", [P, P])
        ld_units = sb("ld_units", [P, H])
        lag = sb("lag", [P, C])
        lag_clamped = sb("lag_clamped", [P, C])
        lag_logdecay = sb("lag_logdecay", [P, H, C])
        lag_decay = sb("lag_decay", [P, H, C])
        decay_mask = sb("decay_mask", [P, 4, 4, 2, C])
        pos_row = sb("pos_row", [P, 2, C])
        q_decay = sb("q_decay", [P, KH, P])
        pos_col = sb("pos_col", [P, 1])
        pos_col64 = sb("pos_col64", [P, 1])
        k_logdecay = sb("k_logdecay", [P, H])
        k_decay = sb("k_decay", [P, H])
        chunk_decay = sb("chunk_decay", [P, KH])
        own_head = sb("own_head", [P, P])
        even_cols = sb("even_cols", [P, 4])
        head_parity = sb("head_parity", [P, 2])
        minus_half = sb("minus_half", [P, H])
        eps_col = sb("eps_col", [P, 1])
        table_load = sb("table_load", [P, 1])

        bn6 = sb("bn6", [P, 2, 6])
        mean_var = sb("mean_var", [P, 2, 2])
        var_eps = sb("var_eps", [P, 2, 1])
        rstd = sb("rstd", [P, 2, 1])
        shift = sb("shift", [P, 2, 1])
        xn = sb("xn", [P, 2, D])
        e4_y = sb("e4_y", [P, D])
        e4_exp = sb("e4_exp", [P, D])
        e4_magic = sb("e4_magic", [P, D])
        e4_sum = sb("e4_sum", [P, D])
        e4_q = sb("e4_q", [P, D], BF16)
        e4_nan = sb("e4_nan", [P, D], BF16)
        xq = sb("xq", [P, 2, D], BF16)
        xT_hi = sb("xT_hi", [P, KH, P], F32R)
        xT_lo = sb("xT_lo", [P, KH, P], F32R)
        xqT = sb("xqT", [P, KH, P], BF16)
        kv = sb("kv", [P, 2, 2 * D])
        kd = sb("kd", [P, 2, D])
        q = sb("q", [P, D])
        g1_stack = sb("g1_stack", [P, P])
        g1T = sb("g1T", [P, P], F32R)
        kT = sb("kT", [P, 2, KH, P])
        qT = sb("qT", [P, 2, KH, 2, P])
        qdT = sb("qdT", [P, 2, KH, P])
        gate_tanh = sb("gate_tanh", [P, 2, D])
        ffn_silu = sb("ffn_silu", [P, 4, D])
        v_parity = sb("v_parity", [P, 2, 2 * (D + E)])
        avT = sb("avT", [P, KH, P])
        probs = sb("probs", [P, 4, 4, 2 * C])
        state = sb("state", [P, KH, C])
        state_c0 = sb("state_c0", [P, 2, KH, P])
        state_c1 = sb("state_c1", [P, KH, P])
        og = sb("og", [P, D])
        og_sq = sb("og_sq", [P, D])
        og_sum = sb("og_sum", [P, H])
        og_var = sb("og_var", [P, H])
        og_rs = sb("og_rs", [P, H])
        og_y2 = sb("og_y2", [P, H])
        og_half = sb("og_half", [P, H])
        on = sb("on", [P, D])
        oT_hi = sb("oT_hi", [P, KH, P], F32R)
        oT_lo = sb("oT_lo", [P, KH, P], F32R)
        sg = sb("sg", [P, D])
        y = sb("y", [P, 2, D])

        def bank(name):
            return ctx.enter_context(nc.psum_tensor(name, [P, 512], F32))

        b_score = [bank("b_score0"), bank("b_score1")]
        b_kv = bank("b_kv")
        b_qg = bank("b_qg")
        b_xo = bank("b_xo")
        b_qk = bank("b_qk")
        b_gate = bank("b_gate")
        b_att = bank("b_att")
        ps_xT = b_xo[:, 0:D].rearrange("p (k t) -> p k t", k=KH)
        ps_oT = b_xo[:, 0:D].rearrange("p (k t) -> p k t", k=KH)
        ps_out = b_xo[:, D:2 * D]
        ps_xqT = b_gate[:, 0:P].bitcast(BF16).rearrange("p (k t) -> p k t", k=KH)
        ps_g1T = b_gate[:, 0:P]
        ps_gate = b_gate[:, 0:D]
        ps_ffn = b_gate[:, D:2 * D]
        ps_qT = b_qk[:, 0:D].rearrange("p (k t) -> p k t", k=KH)
        ps_kT = b_qk[:, D:2 * D].rearrange("p (k t) -> p k t", k=KH)
        ps_state = b_att[:, 0:KH * C].rearrange("p (k c) -> p k c", k=KH)
        ps_o = b_att[:, D:2 * D]
        ps_avT = b_score[0][:, D:2 * D].rearrange("p (k t) -> p k t", k=KH)

        s_x = sem("x_loaded")
        s_w = sem("wk_wv_loaded")
        s_wq = sem("wq_wg1_loaded")
        s_w2 = sem("w2_loaded")
        s_ld = sem("log_decay_loaded")
        s_small = sem("small_loaded")
        s_wo_y = sem("wo_loaded_then_y_stored")
        s_pool = sem("pool_constants")
        s_dvec = sem("dve_constants")
        s_actc = sem("act_constants")
        s_whi = sem("w_hi_ready")
        s_wlo = sem("w_lo_ready")
        s_g2w = sem("wg2_loaded")
        s_g2 = sem("wg2_stack_ready")
        s_woready = sem("wo_parts_ready")
        s_w2q = sem("w2_quant_steps")
        s_w2sum = sem("w2_sum_ready")
        s_lag = sem("lag_ready")
        s_bn = sem("bn_ready")
        s_mv = sem("mean_var_ready")
        s_ve = sem("var_eps_ready")
        s_rstd = sem("rstd_ready")
        s_shift = sem("shift_ready")
        s_xn = sem("xn_ready")
        s_y4 = sem("e4_y_ready")
        s_exp = sem("e4_exp_ready")
        s_e4 = sem("e4_magic_ready")
        s_nan = sem("e4_nan_ready")
        s_e4p = sem("e4_pool_steps")
        s_xq = sem("xq_ready")
        s_xTps = sem("xT_in_psum")
        s_xqTps = sem("xqT_in_psum")
        s_xThi = sem("xT_hi_ready")
        s_xTlo = sem("xT_lo_ready")
        s_xqT = sem("xqT_ready")
        s_kvps = sem("kv_in_psum")
        s_qgps = sem("qg_in_psum")
        s_kv = sem("kv_ready")
        s_q = sem("q_ready")
        s_kd = sem("kd_ready")
        s_g1hi = sem("g1_hi_ready")
        s_g1lo = sem("g1_lo_ready")
        s_g1Tps = sem("g1T_in_psum")
        s_g1T = sem("g1T_ready")
        s_ffnps = sem("ffn_in_psum")
        s_ffn = sem("ffn_silu_ready")
        s_gateps = sem("gate_in_psum")
        s_gate = sem("gate_tanh_ready")
        s_qkTps = sem("qkT_in_psum")
        s_qkT = sem("qkT_ready")
        s_qd = sem("qdT_ready")
        s_score = sem("scores_in_psum")
        s_probs = sem("probs_ready")
        s_kvs = sem("state_step_in_psum")
        s_state = sem("state_ready")
        s_sx = sem("state_masked_ready")
        s_vp = sem("v_parity_ready")
        s_avps = sem("avT_in_psum")
        s_av = sem("avT_ready")
        s_ops = sem("o_in_psum")
        s_og = sem("og_ready")
        s_sq = sem("og_sq_ready")
        s_sum = sem("og_sum_ready")
        s_rs = sem("og_rs_steps")
        s_on = sem("on_ready")
        s_oTps = sem("oT_in_psum")
        s_oThi = sem("oT_hi_ready")
        s_oTlo = sem("oT_lo_ready")
        s_outps = sem("out_in_psum")
        s_sg = sem("sg_ready")
        s_y = sem("y_ready")

        x_v = x.rearrange("b (c p) d -> p (b c) d", p=P)
        out_v = out.rearrange("b (c p) d -> (b c) p d", p=P)

        def need(eng, s, v):
            if not isinstance(v, int) or v > 0:
                eng.wait_ge(s, v)

        def steps(program, prologue):
            def run(eng):
                prologue(eng)
                for j in range(2):
                    program(eng, 0, j)
                with eng.Fori(0, LOOPS) as i:
                    for j in range(2, NB + 2):
                        program(eng, i, j)
                for j in range(2, NB + 2):
                    program(eng, LOOPS, j)
            return run

        def num(i, j):
            return NB * i + j

        def known(i, j):
            return not isinstance(i, int) or NB * i + j in range(G)

        def state_no(i, j, c):
            return (2 * NB - 1) * (i + j // NB) + 2 * (j % NB) + c

        block = ctx.enter_context(nc.Block())

        @block.sync
        def _(sp):
            def prologue(sp):
                sp.dma_start(x_sb[:, 0:1, :], x_v[:, 0:1, :]).then_inc(s_x, 16)
                sp.dma_start(w_f32[:, :, 0:D], Wk.rearrange("(k p) n -> p k n", p=P)).then_inc(s_w, 16)
                sp.dma_start(w_f32[:, :, D:2 * D], Wv.rearrange("(k p) n -> p k n", p=P)).then_inc(s_w, 16)
                sp.dma_start(ld_row[:], log_decay.unsqueeze(0).broadcast_to([P, H])).then_inc(s_ld, 16)
                sp.dma_start(w_f32[:, :, Q0:Q0 + D], Wq.rearrange("(k p) n -> p k n", p=P)).then_inc(s_wq, 16)
                sp.dma_start(w_f32[:, :, 3 * D:NW], Wg1.rearrange("(k p) n -> p k n", p=P)).then_inc(s_wq, 16)
                for half in range(KH):
                    sp.dma_start(ld_col[:, half:half + 1],
                                 log_decay[half * HH:half * HH + HH].unsqueeze(1).broadcast_to([HH, E])).then_inc(s_small, 16)
                sp.dma_start(scales[:, 0:1], scale.unsqueeze(0).broadcast_to([P, 1])).then_inc(s_small, 16)
                sp.dma_start(scales[:, 1:2], scale1.unsqueeze(0).broadcast_to([P, 1])).then_inc(s_small, 16)
                sp.wait_ge(s_x, 16)
                sp.dma_start(x_sb[:, 1:NB, :], x_v[:, 1:NB, :]).then_inc(s_x, 16)
                sp.wait_ge(s_pool, 6)
                for r in range(4):
                    sp.dma_start(wg2_f32[32 * r:32 * r + GR, :], Wg2).then_inc(s_g2w, 16)
                sp.dma_start(w2_f32[:], W2.rearrange("(k p) n -> p k n", p=P)).then_inc(s_w2, 16)
                sp.dma_start(wo_f32[:], Wo.rearrange("(k p) n -> p k n", p=P)).then_inc(s_wo_y, 16)
                for kk in range(KH):
                    sp.dma_start(nw_col[:, kk:kk + 1], norm_w[kk * P:kk * P + P].unsqueeze(1)).then_inc(s_wo_y, 16)
                for b in range(1, B):
                    sp.wait_ge(s_x, 16 * (b + 1))
                    sp.dma_start(x_sb[:, NB * b:NB * b + NB, :], x_v[:, NB * b:NB * b + NB, :]).then_inc(s_x, 16)

            def store(sp, i, j):
                if not known(i, j - 2):
                    return
                sp.wait_ge(s_y, num(i, j - 1))
                dst = out_v[num(i, j - 2)] if isinstance(i, int) else out_v[bass.ds(num(i, j - 2), 1)].rearrange("a p d -> (a p) d")
                sp.dma_start(dst, y[:, j % 2, :]).then_inc(s_wo_y, 16)

            steps(store, prologue)(sp)
            sp.wait_ge(s_wo_y, WO_LOADS + 16 * G)

        @block.gpsimd
        def _(pool):
            g = nc.gpsimd

            def norm_factor(i, j):
                u = j % 2
                pool.wait_ge(s_mv, num(i, j) + 1)
                need(pool, s_xn, num(i, j) - 1)
                g.tensor_tensor(var_eps[:, u], mean_var[:, u, 1:2], eps_col[:], ALU.add).then_inc(s_ve, 1)
                pool.wait_ge(s_ve, num(i, j) + 1)
                g.tensor_tensor(rstd[:, u], var_eps[:, u], minus_half[:, 0:1], ALU.pow).then_inc(s_rstd, 1)

            def round_y(i, j):
                base = 2 * num(i, j)
                pool.wait_ge(s_e4, num(i, j) + 1)
                g.tensor_tensor(e4_sum[:], e4_y[:], e4_magic[:], ALU.add).then_inc(s_e4p, 1)
                pool.wait_ge(s_e4p, base + 1)
                need(pool, s_xq, num(i, j))
                g.tensor_tensor(e4_q[:], e4_sum[:], e4_magic[:], ALU.subtract).then_inc(s_e4p, 1)

            def put_nan(i, j):
                pool.wait_ge(s_nan, num(i, j) + 1)
                need(pool, s_xqTps, num(i, j) - 1)
                g.tensor_tensor(xq[:, j % 2], e4_q[:], e4_nan[:], ALU.add).then_inc(s_xq, 1)

            def decay_k(i, j):
                u = j % 2
                pool.wait_ge(s_kv, num(i, j) + 1)
                need(pool, s_ops, num(i, j) - 1)
                g.tensor_tensor(kd[:, u].rearrange("p (h e) -> p h e", h=H),
                                kv[:, u, 0:D].rearrange("p (h e) -> p h e", h=H),
                                k_decay[:].unsqueeze(2).broadcast_to([P, H, E]), ALU.mult).then_inc(s_kd, 1)

            def spread_state(i, j, c):
                if j % NB == NB - 1 and c == 1:
                    return
                made = state_no(i, j, c) + 1
                pool.wait_ge(s_state, 2 * made)
                dst = state_c1 if c == 0 else state_c0[:, (j + 1) % 2]
                need(pool, s_ops, num(i, j) if c == 0 else num(i, j) - 1)
                g.tensor_tensor(dst[:].rearrange("p k (b c) -> p k b c", b=2),
                                state[:].unsqueeze(2).broadcast_to([P, KH, 2, C]),
                                own_head[:].rearrange("p (b c) -> p b c", b=2).unsqueeze(1).broadcast_to([P, KH, 2, C]),
                                ALU.mult).then_inc(s_sx, 1)

            def head_norm(i, j):
                pool.wait_ge(s_rs, RS_STEPS * (num(i, j) + 1))
                need(pool, s_oTps, num(i, j))
                g.tensor_tensor(on[:].rearrange("p (h e) -> p h e", h=H), og[:].rearrange("p (h e) -> p h e", h=H),
                                og_rs[:].unsqueeze(2).broadcast_to([P, H, E]), ALU.mult).then_inc(s_on, 1)

            def add_x(i, j):
                pool.wait_ge(s_sg, num(i, j) + 1)
                pool.wait_ge(s_wo_y, WO_LOADS + 16 * num(i, j))
                xs = x_sb[:, num(i, j), :] if isinstance(i, int) else x_sb[:, bass.ds(num(i, j), 1), :].rearrange("p a d -> p (a d)")
                g.tensor_tensor(y[:, j % 2, :], sg[:], xs, ALU.add).then_inc(s_y, 1)

            def prologue(pool):
                g.memset(minus_half[:], -0.5)
                g.memset(eps_col[:], EPS).then_inc(s_pool, 1)
                g.memset(ident[:], 0.0).then_inc(s_pool, 1)
                g.memset(ones_row[:], 1.0).then_inc(s_pool, 1)
                g.memset(wg2_f32[:], 0.0).then_inc(s_pool, 1)
                g.memset(g1_stack[:], 0.0).then_inc(s_pool, 1)
                g.memset(wg2_stack[:].bitcast(F32), 0.0).then_inc(s_pool, 1)
                pool.wait_ge(s_pool, 6)
                g.affine_select(out=ident[:], in_=ident[:], compare_op=ALU.not_equal, fill=1.0, base=0,
                                pattern=[[-1, P]], channel_multiplier=1).then_inc(s_pool, 1)
                g.iota(lag[:], pattern=[[1, C]], base=0, channel_multiplier=-1, allow_small_or_imprecise_dtypes=True).then_inc(s_pool, 1)
                g.iota(pos_row[:], pattern=[[0, 2], [1, C]], base=1, channel_multiplier=0, allow_small_or_imprecise_dtypes=True).then_inc(s_pool, 1)
                g.iota(pos_col64[:], pattern=[[0, 1]], base=2 * C - 1, channel_multiplier=-1, allow_small_or_imprecise_dtypes=True).then_inc(s_pool, 1)
                norm_factor(0, 0)
                pool.wait_ge(s_rstd, 1)
                g.tensor_scalar(lag[C:P], lag[C:P], float(C), 1.0, ALU.add, ALU.mult).then_inc(s_lag, 1)
                pool.wait_ge(s_lag, 1)
                g.tensor_scalar(pos_col[0:C], pos_col64[0:C], -float(C), 1.0, ALU.add, ALU.mult).then_inc(s_pool, 1)
                pool.wait_ge(s_pool, 11)
                g.tensor_scalar(pos_col[C:P], pos_col64[C:P], 1.0, 0.0, ALU.mult, ALU.add).then_inc(s_pool, 1)
                pool.wait_ge(s_pool, 12)
                g.memset(decay_mask[:], 0.0)
                g.affine_select(out=even_cols[:], in_=ones_row[:, 0:4], compare_op=ALU.is_ge, fill=0.0, base=0,
                                pattern=[[-2 * E, 4]], channel_multiplier=1).then_inc(s_pool, 1)
                pool.wait_ge(s_pool, 13)
                g.affine_select(out=even_cols[:], in_=even_cols[:], compare_op=ALU.is_ge, fill=0.0, base=E - 1,
                                pattern=[[2 * E, 4]], channel_multiplier=-1).then_inc(s_pool, 1)
                g.memset(v_parity[:], 0.0).then_inc(s_pool, 1)
                g.affine_select(out=own_head[:].rearrange("p (h e) -> p h e", h=HH), in_=ones_row[:].rearrange("p (h e) -> p h e", h=HH),
                                compare_op=ALU.is_ge, fill=0.0, base=0, pattern=[[-E, HH], [0, E]], channel_multiplier=1).then_inc(s_pool, 1)
                pool.wait_ge(s_pool, 16)
                g.affine_select(out=own_head[:].rearrange("p (h e) -> p h e", h=HH), in_=own_head[:].rearrange("p (h e) -> p h e", h=HH),
                                compare_op=ALU.is_ge, fill=0.0, base=E - 1, pattern=[[E, HH], [0, E]], channel_multiplier=-1).then_inc(s_pool, 1)
                pool.wait_ge(s_actc, 1)
                dm = decay_mask[:].rearrange("p r i b c -> p (r i) b c")
                for c in range(2):
                    pool.wait_ge(s_pool, 17 + c)
                    if c == 1:
                        norm_factor(0, 1)
                        pool.wait_ge(s_rstd, 2)
                    g.affine_select(out=dm[c * C:c * C + C, :, c, :], in_=lag_decay[c * C:c * C + C], compare_op=ALU.is_ge,
                                    fill=0.0, base=0, pattern=[[0, H], [1, C]], channel_multiplier=-1).then_inc(s_pool, 1)
                pool.wait_ge(s_pool, 19)
                pool.wait_ge(s_actc, 5)
                decay_k(0, 0)
                round_y(0, 0)
                norm_factor(0, 2)
                pool.wait_ge(s_w2q, 3)
                g.tensor_tensor(w2_m[:], w2_y[:], w2_f32[:], ALU.add).then_inc(s_w2sum, 1)

            def step(pool, i, j):
                nxt, cur, norm = known(i, j + 1), known(i, j), known(i, j + 2)
                first = isinstance(i, int) and num(i, j) == 0
                if first:
                    put_nan(0, 0)
                if nxt:
                    round_y(i, j + 1)
                if norm and not first:
                    norm_factor(i, j + 2)
                if nxt:
                    put_nan(i, j + 1)
                if cur:
                    spread_state(i, j, 0)
                if known(i, j - 2) and known(i, j - 1):
                    add_x(i, j - 2)
                if nxt:
                    decay_k(i, j + 1)
                if known(i, j - 1) and cur:
                    head_norm(i, j - 1)
                if cur:
                    spread_state(i, j, 1)

            steps(step, prologue)(pool)

        @block.scalar
        def _(act):
            a = nc.scalar

            def high_xT(i, j):
                act.wait_ge(s_xTps, num(i, j) + 1)
                need(act, s_qgps, num(i, j))
                a.activation(xT_hi[:], ps_xT, ACT.Copy).then_inc(s_xThi, 1)

            def copy_xqT(i, j):
                act.wait_ge(s_xqTps, num(i, j) + 1)
                need(act, s_ffnps, num(i, j))
                a.activation(xqT[:], ps_xqT, ACT.Copy).then_inc(s_xqT, 1)

            def silu_kv(i, j):
                act.wait_ge(s_kvps, num(i, j) + 1)
                need(act, s_ops, num(i, j) - 1)
                need(act, s_kd, num(i, j) - 1)
                a.activation(kv[:, j % 2], b_kv[:], ACT.Silu).then_inc(s_kv, 1)

            def silu_q(i, j):
                act.wait_ge(s_qgps, num(i, j) + 1)
                need(act, s_qkTps, num(i, j))
                a.activation(q[:], b_qg[:, 0:D], ACT.Silu).then_inc(s_q, 1)
                need(act, s_g1Tps, num(i, j))
                a.activation(g1_stack[:, 0:64].bitcast(F32R).rearrange("p (r c) -> p r c", r=2)[:, :, 0:GR],
                             b_qg[:, D:D + GR].unsqueeze(1).broadcast_to([P, 2, GR]), ACT.Copy).then_inc(s_g1hi, 1)

            def silu_ffn(i, j):
                act.wait_ge(s_ffnps, num(i, j) + 1)
                need(act, s_sg, num(i, j) - 2)
                a.activation(ffn_silu[:, j % 4], ps_ffn, ACT.Silu, scale=descale[:, 0:1]).then_inc(s_ffn, 1)

            def copy_g1T(i, j):
                act.wait_ge(s_g1Tps, num(i, j) + 1)
                need(act, s_gateps, num(i, j))
                a.activation(g1T[:], ps_g1T, ACT.Copy).then_inc(s_g1T, 1)

            def copy_kT(i, j):
                u = j % 2
                act.wait_ge(s_qkTps, num(i, j) + 1)
                need(act, s_score, 4 * (num(i, j) - 1))
                a.activation(kT[:, u], ps_kT, ACT.Copy).then_inc(s_qkT, 1)

            def copy_qT(i, j):
                u = j % 2
                for par in range(2):
                    a.activation(qT[:, u, :, par, :], ps_qT, ACT.Copy, scale=head_parity[:, par:par + 1]).then_inc(s_qkT, 1)

            def gate(i, j):
                act.wait_ge(s_gateps, num(i, j) + 1)
                need(act, s_og, num(i, j) - 1)
                a.activation(gate_tanh[:, j % 2], ps_gate, ACT.Tanh, scale=0.5).then_inc(s_gate, 1)

            def high_oT(i, j):
                act.wait_ge(s_oTps, num(i, j) + 1)
                need(act, s_outps, num(i, j))
                a.activation(oT_hi[:], ps_oT, ACT.Copy).then_inc(s_oThi, 1)

            def normalise(i, j):
                u = j % 2
                act.wait_ge(s_shift, num(i, j) + 1)
                need(act, s_xTps, num(i, j) - 1)
                xs = x_sb[:, num(i, j), :] if isinstance(i, int) else x_sb[:, bass.ds(num(i, j), 1), :].rearrange("p a d -> p (a d)")
                a.activation(xn[:, u], xs, ACT.Identity, bias=shift[:, u, 0:1], scale=rstd[:, u, 0:1]).then_inc(s_xn, 1)

            def part_v(i, j):
                u = j % 2
                act.wait_ge(s_kv, num(i, j) + 1)
                need(act, s_avps, num(i, j) - 1)
                dst = v_parity[:, u].rearrange("p (q c) -> p q c", q=2)[:, :, 0:D].rearrange("p q (a b e) -> p q a b e", a=HH, b=2)[:, :, :, 0, :]
                src = kv[:, u, D:2 * D].rearrange("p (a b e) -> p b a e", a=HH, b=2)
                a.activation(dst, src, ACT.Copy).then_inc(s_vp, 1)

            def scale_y(i, j):
                act.wait_ge(s_xn, num(i, j) + 1)
                need(act, s_e4p, 2 * num(i, j))
                a.activation(e4_y[:], xn[:, j % 2], ACT.Copy, scale=scales[:, 0:1]).then_inc(s_y4, 1)

            def square_o(i, j):
                act.wait_ge(s_og, num(i, j) + 1)
                need(act, s_sum, num(i, j))
                a.activation(og_sq[:], og[:], ACT.Square).then_inc(s_sq, 1)

            def copy_avT(i, j):
                act.wait_ge(s_avps, num(i, j) + 1)
                need(act, s_ops, num(i, j))
                a.activation(avT[:], ps_avT, ACT.Copy).then_inc(s_av, 1)

            def high_w(a0, b0):
                for kk in range(KH):
                    a.activation(w_hi[:, kk, a0:b0], w_f32[:, kk, a0:b0], ACT.Copy).then_inc(s_whi, 1)

            def prologue(act):
                act.wait_ge(s_pool, 1)
                a.activation(table_load[:], eps_col[:], ACT.Exp)
                act.wait_ge(s_w, 32)
                high_w(0, Q0)
                normalise(0, 0)
                act.wait_ge(s_dvec, 3)
                a.activation(lag_decay[:], lag_logdecay[:], ACT.Exp).then_inc(s_actc, 1)
                high_xT(0, 0)
                act.wait_ge(s_small, 64)
                for half in range(KH):
                    a.activation(q_decay[:, half], pos_row[:].rearrange("p b c -> p (b c)"), ACT.Exp,
                                 scale=ld_col[:, half:half + 1]).then_inc(s_actc, 1)
                a.activation(k_decay[:], k_logdecay[:], ACT.Exp).then_inc(s_actc, 1)
                a.activation(chunk_decay[:], ld_col[:], ACT.Exp, scale=float(C)).then_inc(s_actc, 1)
                a.activation(table_load[:], eps_col[:], ACT.Silu)
                silu_kv(0, 0)
                silu_q(0, 0)
                scale_y(0, 0)
                act.wait_ge(s_dvec, 7)
                copy_kT(0, 0)
                copy_qT(0, 0)
                copy_g1T(0, 0)
                high_xT(0, 1)
                act.wait_ge(s_pool, 15)
                part_v(0, 0)
                scale_y(0, 1)

            def step(act, i, j):
                nxt, cur, norm = known(i, j + 1), known(i, j), known(i, j + 2)
                if cur:
                    gate(i, j)
                first = isinstance(i, int) and num(i, j) == 0
                if norm:
                    normalise(i, j + 2)
                if nxt:
                    silu_kv(i, j + 1)
                if first:
                    copy_xqT(0, 0)
                if nxt:
                    silu_q(i, j + 1)
                if first:
                    silu_ffn(0, 0)
                if nxt:
                    part_v(i, j + 1)
                if first:
                    act.wait_ge(s_woready, 2)
                    a.activation(wo_hi[:], wo_scaled[:], ACT.Copy).then_inc(s_woready, 1)
                if nxt:
                    copy_xqT(i, j + 1)
                if norm:
                    high_xT(i, j + 2)
                if nxt:
                    copy_kT(i, j + 1)
                    copy_qT(i, j + 1)
                if cur:
                    copy_avT(i, j)
                if nxt:
                    silu_ffn(i, j + 1)
                if norm:
                    scale_y(i, j + 2)
                if known(i, j - 1):
                    high_oT(i, j - 1)
                if nxt:
                    copy_g1T(i, j + 1)
                if cur:
                    square_o(i, j)

            steps(step, prologue)(act)

        @block.vector
        def _(dve):
            v = nc.vector

            def stats(i, j):
                u = j % 2
                if isinstance(i, int) and NB * i + j == 0:
                    dve.wait_ge(s_x, 16)
                else:
                    dve.wait_ge(s_x, 16 * (i + j // NB) + 32)
                xs = x_sb[:, num(i, j), :] if isinstance(i, int) else x_sb[:, bass.ds(num(i, j), 1), :].rearrange("p a d -> p (a d)")
                v.bn_stats(bn6[:, u], xs).then_inc(s_bn, 1)

            def aggregate_waits(i, j):
                dve.wait_ge(s_bn, num(i, j) + 1)
                need(dve, s_ve, num(i, j) - 1)

            def aggregate(i, j):
                u = j % 2
                v.bn_aggr(mean_var[:, u], bn6[:, u]).then_inc(s_mv, 1)

            def shift_x(i, j):
                u = j % 2
                dve.wait_ge(s_mv, num(i, j) + 1)
                dve.wait_ge(s_rstd, num(i, j) + 1)
                need(dve, s_xn, num(i, j) - 1)
                v.scalar_tensor_tensor(out=shift[:, u], in0=mean_var[:, u, 0:1], scalar=-1.0, in1=rstd[:, u],
                                       op0=ALU.mult, op1=ALU.mult).then_inc(s_shift, 1)

            def exponent(i, j):
                dve.wait_ge(s_y4, num(i, j) + 1)
                need(dve, s_e4p, 2 * num(i, j))
                v.tensor_scalar(e4_exp[:].bitcast(I32), e4_y[:].bitcast(I32), 0x7F800000, None, ALU.bitwise_and).then_inc(s_exp, 1)

            def magic(i, j):
                dve.wait_ge(s_exp, num(i, j) + 1)
                v.tensor_scalar(e4_magic[:], e4_exp[:], E4_MIN, E4_MAGIC, ALU.max, ALU.mult).then_inc(s_e4, 1)

            def find_nan(i, j):
                dve.wait_ge(s_e4p, 2 * (num(i, j) + 1))
                need(dve, s_xq, num(i, j))
                v.tensor_scalar(e4_nan[:], e4_q[:], E4_OVER, 0.0, ALU.mult, ALU.mult).then_inc(s_nan, 1)

            def low_xT(i, j):
                dve.wait_ge(s_xThi, num(i, j) + 1)
                need(dve, s_qgps, num(i, j))
                v.tensor_tensor(xT_lo[:], ps_xT, xT_hi[:].bitcast(F32), ALU.subtract).then_inc(s_xTlo, 1)

            def low_g1(i, j):
                dve.wait_ge(s_g1hi, num(i, j) + 1)
                v.tensor_tensor(g1_stack[:, 64:128].bitcast(F32R).rearrange("p (r c) -> p r c", r=2)[:, :, 0:GR],
                                b_qg[:, D:D + GR].unsqueeze(1).broadcast_to([P, 2, GR]),
                                g1_stack[:, 0:64].rearrange("p (r c) -> p r c", r=2)[:, :, 0:GR],
                                ALU.subtract).then_inc(s_g1lo, 1)

            def mask(i, j, r):
                dve.wait_ge(s_score, 4 * num(i, j) + r + 1)
                need(dve, s_ops, num(i, j))
                v.tensor_tensor(probs[:, r].rearrange("p i (b c) -> p i b c", b=2),
                                b_score[r % 2][:, 0:4 * C].rearrange("p (i c) -> p i c", i=4).unsqueeze(2).broadcast_to([P, 4, 2, C]),
                                decay_mask[:, r], ALU.mult).then_inc(s_probs, 1)

            def add_state(i, j, c):
                if j % NB == NB - 1 and c == 1:
                    return
                dve.wait_ge(s_kvs, state_no(i, j, c) + 1)
                if j % NB == 0 and c == 0:
                    need(dve, s_sx, state_no(i, j, c))
                    v.tensor_copy(state[:], ps_state).then_inc(s_state, 2)
                else:
                    dve.wait_ge(s_state, 2 * state_no(i, j, c))
                    dve.wait_ge(s_sx, state_no(i, j, c))
                    for half in range(KH):
                        v.scalar_tensor_tensor(out=state[:, half], in0=state[:, half], scalar=chunk_decay[:, half:half + 1],
                                               in1=ps_state[:, half], op0=ALU.mult, op1=ALU.add).then_inc(s_state, 1)

            def decay_q(i, j):
                dve.wait_ge(s_qkT, 3 * (num(i, j) + 1))
                need(dve, s_ops, num(i, j) - 1)
                v.tensor_tensor(qdT[:, j % 2], ps_qT, q_decay[:], ALU.mult).then_inc(s_qd, 1)

            def gate_o(i, j):
                dve.wait_ge(s_ops, num(i, j) + 1)
                dve.wait_ge(s_gate, num(i, j) + 1)
                need(dve, s_on, num(i, j))
                v.scalar_tensor_tensor(out=og[:], in0=gate_tanh[:, j % 2], scalar=1.0, in1=ps_o,
                                       op0=ALU.add, op1=ALU.mult).then_inc(s_og, 1)

            def sum_heads(i, j):
                dve.wait_ge(s_sq, num(i, j) + 1)
                need(dve, s_rs, RS_STEPS * num(i, j))
                v.tensor_reduce(og_sum[:], og_sq[:].rearrange("p (h e) -> p h e", h=H), AX_X, ALU.add).then_inc(s_sum, 1)

            def rsqrt(i, j, first, last):
                for m in range(first, last):
                    if m == 0:
                        dve.wait_ge(s_sum, num(i, j) + 1)
                        need(dve, s_on, num(i, j))
                    else:
                        dve.wait_ge(s_rs, RS_STEPS * num(i, j) + m)
                    if m == 0:
                        ins = v.tensor_scalar(og_var[:], og_sum[:], 1.0 / E, 4.0 * EPS, ALU.mult, ALU.add)
                    elif m == 1:
                        ins = v.tensor_scalar(og_half[:].bitcast(I32), og_var[:].bitcast(I32), 1, None, ALU.logical_shift_right)
                    elif m == 2:
                        ins = v.tensor_scalar(og_rs[:].bitcast(I32), og_half[:].bitcast(I32), -1.0, float(0x5F3759DF), ALU.mult, ALU.add)
                    elif m % 3 == 0:
                        ins = v.tensor_tensor(og_y2[:], og_rs[:], og_rs[:], ALU.mult)
                    elif m % 3 == 1:
                        ins = v.scalar_tensor_tensor(out=og_half[:], in0=og_y2[:], scalar=-0.5, in1=og_var[:], op0=ALU.mult, op1=ALU.mult)
                    else:
                        ins = v.scalar_tensor_tensor(out=og_rs[:], in0=og_half[:], scalar=1.5, in1=og_rs[:], op0=ALU.add, op1=ALU.mult)
                    ins.then_inc(s_rs, 1)

            def low_oT(i, j):
                dve.wait_ge(s_oThi, num(i, j) + 1)
                need(dve, s_outps, num(i, j))
                v.tensor_tensor(oT_lo[:], ps_oT, oT_hi[:].bitcast(F32), ALU.subtract).then_inc(s_oTlo, 1)

            def product(i, j):
                dve.wait_ge(s_outps, num(i, j) + 1)
                dve.wait_ge(s_ffn, num(i, j) + 1)
                v.tensor_tensor(sg[:], ps_out, ffn_silu[:, j % 4], ALU.mult).then_inc(s_sg, 1)

            def head_norm_last(i, j):
                dve.wait_ge(s_rs, RS_STEPS * (num(i, j) + 1))
                dve.wait_ge(s_oTps, num(i, j))
                v.tensor_tensor(on[:].rearrange("p (h e) -> p h e", h=H), og[:].rearrange("p (h e) -> p h e", h=H),
                                og_rs[:].unsqueeze(2).broadcast_to([P, H, E]), ALU.mult).then_inc(s_on, 1)

            def add_x_last(i, j):
                dve.wait_ge(s_sg, num(i, j) + 1)
                dve.wait_ge(s_wo_y, WO_LOADS + 16 * num(i, j))
                v.tensor_tensor(y[:, j % 2, :], sg[:], x_sb[:, num(i, j), :], ALU.add).then_inc(s_y, 1)

            def low_w(a0, b0, first):
                for kk in range(KH):
                    dve.wait_ge(s_whi, first + kk + 1)
                    v.tensor_tensor(w_lo[:, kk, a0:b0], w_f32[:, kk, a0:b0], w_hi[:, kk, a0:b0].bitcast(F32), ALU.subtract).then_inc(s_wlo, 1)

            def quantise_w2():
                dve.wait_ge(s_w2, 16)
                v.tensor_scalar(w2_y[:], w2_f32[:], scales[:, 1:2], None, ALU.mult).then_inc(s_w2q, 1)
                dve.wait_ge(s_w2q, 1)
                v.tensor_scalar(w2_m[:].bitcast(I32), w2_y[:].bitcast(I32), 0x7F800000, None, ALU.bitwise_and).then_inc(s_w2q, 1)
                dve.wait_ge(s_w2q, 2)
                v.tensor_scalar(w2_f32[:], w2_m[:], E4_MIN, E4_MAGIC, ALU.max, ALU.mult).then_inc(s_w2q, 1)

            def finish_w2():
                dve.wait_ge(s_w2sum, 1)
                v.tensor_tensor(w2_q[:], w2_m[:], w2_f32[:], ALU.subtract).then_inc(s_w2q, 1)
                dve.wait_ge(s_w2q, 4)
                v.tensor_scalar(w2_nan[:], w2_q[:], E4_OVER, 0.0, ALU.mult, ALU.mult).then_inc(s_w2q, 1)
                dve.wait_ge(s_w2q, 5)
                v.tensor_tensor(w2_fp8[:], w2_q[:], w2_nan[:], ALU.add).then_inc(s_w2q, 1)

            def scale_wo():
                dve.wait_ge(s_wo_y, WO_LOADS)
                for kk in range(KH):
                    v.tensor_scalar(wo_scaled[:, kk], wo_f32[:, kk], nw_col[:, kk:kk + 1], None, ALU.mult).then_inc(s_woready, 1)

            def low_wo():
                dve.wait_ge(s_woready, 3)
                v.tensor_tensor(wo_lo[:], wo_scaled[:], wo_hi[:].bitcast(F32), ALU.subtract).then_inc(s_woready, 1)

            def prologue(dve):
                stats(0, 0)
                aggregate_waits(0, 0)
                aggregate(0, 0)
                dve.wait_ge(s_ld, 16)
                v.tensor_copy(ld_units[:].rearrange("p (r k q) -> p r k q", r=4, k=2),
                              ld_row[:].rearrange("p (k r q) -> p r k q", k=2, r=4)).then_inc(s_dvec, 1)
                shift_x(0, 0)
                dve.wait_ge(s_lag, 1)
                v.tensor_scalar(lag_clamped[:], lag[:], 0.0, None, ALU.max).then_inc(s_dvec, 1)
                dve.wait_ge(s_dvec, 2)
                v.tensor_tensor(lag_logdecay[:], lag_clamped[:].unsqueeze(1).broadcast_to([P, H, C]),
                                ld_units[:].unsqueeze(2).broadcast_to([P, H, C]), ALU.mult)
                dve.wait_ge(s_pool, 12)
                v.tensor_scalar(k_logdecay[:], ld_row[:], pos_col[:, 0:1], None, ALU.mult).then_inc(s_dvec, 1)
                low_w(0, Q0, 0)
                low_xT(0, 0)
                dve.wait_ge(s_wq, 32)
                for kk in range(KH):
                    v.tensor_copy(w_hi[:, kk, Q0:NW], w_f32[:, kk, Q0:NW]).then_inc(s_whi, 1)
                low_w(Q0, NW, 2)
                stats(0, 1)
                aggregate_waits(0, 1)
                aggregate(0, 1)
                v.tensor_copy(ident_bf[:], ident[:]).then_inc(s_dvec, 1)
                dve.wait_ge(s_small, 64)
                v.reciprocal(inv_scales[:], scales[:]).then_inc(s_dvec, 1)
                dve.wait_ge(s_pool, 14)
                v.tensor_reduce(head_parity[:, 0:1], even_cols[:], AX_X, ALU.add).then_inc(s_dvec, 1)
                dve.wait_ge(s_dvec, 6)
                v.tensor_scalar(descale[:], inv_scales[:, 0:1], inv_scales[:, 1:2], None, ALU.mult)
                v.tensor_scalar(head_parity[:, 1:2], head_parity[:, 0:1], -1.0, 1.0, ALU.mult, ALU.add).then_inc(s_dvec, 1)
                shift_x(0, 1)
                low_g1(0, 0)
                dve.wait_ge(s_shift, 2)
                v.tensor_scalar(xn[:, 1], x_sb[:, 1, :], rstd[:, 1, 0:1], shift[:, 1, 0:1], ALU.mult, ALU.add).then_inc(s_xn, 1)
                dve.wait_ge(s_g2w, 64)
                dve.wait_ge(s_pool, 6)
                v.tensor_copy(wg2_hi[:], wg2_f32[:]).then_inc(s_g2, 1)
                exponent(0, 0)
                dve.wait_ge(s_g2, 1)
                for r in range(4):
                    rows = slice(32 * r, 32 * r + GR)
                    if r % 2 == 0:
                        v.tensor_copy(wg2_stack[rows], wg2_f32[rows]).then_inc(s_g2, 1)
                    else:
                        v.tensor_tensor(wg2_stack[rows], wg2_f32[rows], wg2_hi[rows].bitcast(F32), ALU.subtract).then_inc(s_g2, 1)
                magic(0, 0)
                stats(0, 2)
                aggregate_waits(0, 2)
                aggregate(0, 2)
                dve.wait_ge(s_actc, 5)
                decay_q(0, 0)
                low_xT(0, 1)
                quantise_w2()
                dve.wait_ge(s_pool, 19)

            def step(dve, i, j):
                nxt, cur, norm = known(i, j + 1), known(i, j), known(i, j + 2)
                back = known(i, j - 1)
                first = isinstance(i, int) and num(i, j) == 0

                def newton(a0, b0):
                    if back:
                        rsqrt(i, j - 1, a0, b0)

                if not cur:
                    if back:
                        sum_heads(i, j - 1)
                        newton(0, 8)
                    else:
                        dve.wait_ge(s_y, G - 1)
                    product(i, j - 2)
                    if back:
                        newton(8, RS_STEPS)
                        head_norm_last(i, j - 1)
                        low_oT(i, j - 1)
                    else:
                        add_x_last(i, j - 2)
                    return
                if not nxt:
                    mask(i, j, 0)
                    mask(i, j, 1)
                    add_state(i, j, 0)
                    mask(i, j, 2)
                    mask(i, j, 3)
                    sum_heads(i, j - 1)
                    newton(0, 2)
                    product(i, j - 2)
                    newton(2, RS_STEPS)
                    gate_o(i, j)
                    low_oT(i, j - 1)
                    return
                if cur:
                    mask(i, j, 0)
                if first:
                    shift_x(0, 2)
                if norm and not first:
                    stats(i, j + 2)
                if back:
                    sum_heads(i, j - 1)
                if norm and not first:
                    aggregate_waits(i, j + 2)
                if cur:
                    mask(i, j, 1)
                if norm and not first:
                    aggregate(i, j + 2)
                if first:
                    find_nan(0, 0)
                    exponent(0, 1)
                    magic(0, 1)
                    add_state(0, 0, 0)
                    finish_w2()
                newton(0, 1)
                if nxt:
                    find_nan(i, j + 1)
                newton(1, 2)
                if known(i, j - 2):
                    product(i, j - 2)
                newton(2, 4)
                if norm and not first:
                    shift_x(i, j + 2)
                newton(4, 5)
                if cur and not first:
                    add_state(i, j, 0)
                newton(5, 6)
                if first:
                    scale_wo()
                if cur:
                    mask(i, j, 2)
                newton(6, 8)
                if cur:
                    mask(i, j, 3)
                newton(8, 9)
                if cur:
                    add_state(i, j, 1)
                newton(9, 10)
                if nxt:
                    low_g1(i, j + 1)
                newton(10, RS_STEPS)
                if norm:
                    low_xT(i, j + 2)
                if first:
                    low_wo()
                if nxt:
                    decay_q(i, j + 1)
                if norm:
                    exponent(i, j + 2)
                if known(i, j - 2):
                    dve.wait_ge(s_y, num(i, j - 1))
                if norm:
                    magic(i, j + 2)
                if cur:
                    gate_o(i, j)
                if back:
                    low_oT(i, j - 1)

            steps(step, prologue)(dve)

        @block.tensor
        def _(pe):
            t = nc.tensor

            def transpose_x(i, j):
                u = j % 2
                pe.wait_ge(s_xn, num(i, j) + 1)
                need(pe, s_sg, num(i, j) - 3)
                for kk in range(KH):
                    mm = t.transpose(ps_xT[:, kk, :], xn[:, u, kk * P:kk * P + P], ident[:])
                mm.then_inc(s_xTps, 1)

            def transpose_xq(i, j):
                u = j % 2
                pe.wait_ge(s_xq, num(i, j) + 1)
                need(pe, s_gate, max(num(i, j), 1) if isinstance(i, int) else num(i, j))
                if isinstance(i, int) and num(i, j) == 1:
                    pe.wait_ge(s_ffn, 1)
                for kk in range(KH):
                    mm = t.transpose(ps_xqT[:, kk, :], xq[:, u, kk * P:kk * P + P], ident_bf[:])
                mm.then_inc(s_xqTps, 1)

            def project(i, j, dst, a, b, s_done, s_free, free):
                pe.wait_ge(s_xThi, num(i, j) + 1)
                need(pe, s_free, free)
                for kk in range(KH):
                    t.matmul(dst, xT_hi[:, kk], w_hi[:, kk, a:b], start=(kk == 0), stop=False)
                for kk in range(KH):
                    t.matmul(dst, xT_hi[:, kk], w_lo[:, kk, a:b], start=False, stop=False)
                pe.wait_ge(s_xTlo, num(i, j) + 1)
                for kk in range(KH):
                    mm = t.matmul(dst, xT_lo[:, kk], w_hi[:, kk, a:b], start=False, stop=(kk == KH - 1))
                mm.then_inc(s_done, 1)

            def project_kv(i, j):
                project(i, j, b_kv[:, :], 0, 2 * D, s_kvps, s_kv, num(i, j))

            def project_qg(i, j):
                project(i, j, b_qg[:, 0:NW - Q0], Q0, NW, s_qgps, s_g1lo, num(i, j))

            def ffn(i, j):
                pe.wait_ge(s_xqT, num(i, j) + 1)
                for kk in range(KH):
                    mm = t.matmul(ps_ffn, xqT[:, kk], w2_fp8[:, kk], start=(kk == 0), stop=(kk == KH - 1))
                mm.then_inc(s_ffnps, 1)

            def transpose_g1(i, j):
                pe.wait_ge(s_g1lo, num(i, j) + 1)
                if not isinstance(i, int) or num(i, j) > 0:
                    pe.wait_ge(s_ffn, num(i, j) + 1)
                t.transpose(ps_g1T, g1_stack[:], ident[:]).then_inc(s_g1Tps, 1)

            def transpose_qk(i, j):
                pe.wait_ge(s_kv, num(i, j) + 1)
                pe.wait_ge(s_q, num(i, j) + 1)
                need(pe, s_qd, num(i, j))
                for kk in range(KH):
                    t.transpose(ps_qT[:, kk, :], q[:, kk * P:kk * P + P], ident[:])
                for kk in range(KH):
                    mm = t.transpose(ps_kT[:, kk, :], kv[:, j % 2, kk * P:kk * P + P], ident[:])
                mm.then_inc(s_qkTps, 1)

            def gate(i, j):
                pe.wait_ge(s_g1T, num(i, j) + 1)
                t.matmul(ps_gate, g1T[:], wg2_stack[:], start=True, stop=True).then_inc(s_gateps, 1)

            def scores(i, j, r):
                u = j % 2
                if r == 0:
                    pe.wait_ge(s_qkT, 3 * (num(i, j) + 1))
                    need(pe, s_av, num(i, j))
                need(pe, s_probs, 4 * num(i, j) + r - 1)
                rows = slice(32 * r, 32 * r + 32)
                for half in range(KH):
                    for c in range(2):
                        mm = t.matmul(b_score[r % 2][c * C:c * C + C, half * 2 * C:(half + 1) * 2 * C],
                                      kT[rows, u, half, c * C:c * C + C], qT[rows, u, half, :, c * C:c * C + C],
                                      start=True, stop=True)
                mm.then_inc(s_score, 1)

            def state_waits(i, j, c):
                if j % NB == NB - 1 and c == 1:
                    return
                if c == 0:
                    pe.wait_ge(s_kd, num(i, j) + 1)
                    need(pe, s_og, num(i, j))
                else:
                    pe.wait_ge(s_state, 2 * state_no(i, j, 1))

            def state_step(i, j, c):
                if j % NB == NB - 1 and c == 1:
                    return
                u = j % 2
                rows = slice(c * C, c * C + C)
                for half in range(KH):
                    for b in range(2):
                        cols = slice(half * P + b * C, half * P + b * C + C)
                        mm = t.matmul(ps_state[b * C:b * C + C, half, :], kd[rows, u, cols],
                                      kv[rows, u, D + cols.start:D + cols.stop], start=True, stop=True)
                mm.then_inc(s_kvs, 1)

            def from_chunk(i, j):
                u = j % 2
                pe.wait_ge(s_probs, 4 * (num(i, j) + 1))
                pe.wait_ge(s_vp, num(i, j) + 1)
                for half in range(KH):
                    for par in range(2):
                        for r in range(4):
                            mm = t.matmul(ps_avT[32 * r:32 * r + 32, half, :],
                                          v_parity[:, u, par * D + half * P + 32 * r:par * D + half * P + 32 * r + 32],
                                          probs[:, r, 2 * half + par, :], start=(par == 0), stop=(par == 1),
                                          skip_group_check=True)
                mm.then_inc(s_avps, 1)

            def from_state(i, j):
                u = j % 2
                pe.wait_ge(s_qd, num(i, j) + 1)
                pe.wait_ge(s_sx, state_no(i, j, 1))
                if j % NB == NB - 1:
                    pe.wait_ge(s_state, 2 * state_no(i, j, 1))
                else:
                    pe.wait_ge(s_state, 2 * state_no(i, j, 1) + 2)
                for c in range(1 if j % NB == 0 else 0, 2):
                    st = state_c0[:, u] if c == 0 else state_c1
                    for half in range(KH):
                        t.matmul(ps_o[c * C:c * C + C, half * P:half * P + P], qdT[:, u, half, c * C:c * C + C],
                                 st[:, half, :], start=(half == 0), stop=False, skip_group_check=True)

            def add_chunk(i, j):
                first = j % NB == 0
                pe.wait_ge(s_av, num(i, j) + 1)
                if first:
                    for half in range(KH):
                        t.matmul(ps_o[0:C, half * P:half * P + P], avT[:, half, 0:C], ident[:],
                                 start=(half == 0), stop=True, skip_group_check=True)
                    for half in range(KH):
                        mm = t.matmul(ps_o[C:P, half * P:half * P + P], avT[:, half, C:P], ident[:],
                                      start=False, stop=True, skip_group_check=True)
                else:
                    for half in range(KH):
                        mm = t.matmul(ps_o[:, half * P:half * P + P], avT[:, half, :], ident[:],
                                      start=False, stop=True, skip_group_check=True)
                mm.then_inc(s_ops, 1)

            def transpose_o(i, j):
                pe.wait_ge(s_on, num(i, j) + 1)
                if known(i, j + 3):
                    pe.wait_ge(s_xTlo, num(i, j) + 4)
                else:
                    pe.wait_ge(s_sg, num(i, j))
                for kk in range(KH):
                    mm = t.transpose(ps_oT[:, kk, :], on[:, kk * P:kk * P + P], ident[:])
                mm.then_inc(s_oTps, 1)

            def project_o(i, j):
                pe.wait_ge(s_oTlo, num(i, j) + 1)
                parts = [(oT_hi, wo_hi), (oT_hi, wo_lo), (oT_lo, wo_hi)]
                for n, (lhs, rhs) in enumerate(parts):
                    for kk in range(KH):
                        mm = t.matmul(ps_out, lhs[:, kk], rhs[:, kk], start=(n == 0 and kk == 0), stop=(n == 2 and kk == KH - 1))
                mm.then_inc(s_outps, 1)

            def keep_warm(count):
                for _ in range(count):
                    t.matmul(b_score[1][:, 0:P], ident[:], ident[:], start=True, stop=True)

            def prologue(pe):
                pe.wait_ge(s_pool, 7)
                keep_warm(11)
                transpose_x(0, 0)
                keep_warm(3)
                pe.wait_ge(s_wlo, 2)
                project_kv(0, 0)
                pe.wait_ge(s_wlo, 4)
                project_qg(0, 0)
                transpose_qk(0, 0)
                transpose_g1(0, 0)
                transpose_x(0, 1)
                keep_warm(3)
                pe.wait_ge(s_dvec, 4)

            def step(pe, i, j):
                nxt, cur, norm = known(i, j + 1), known(i, j), known(i, j + 2)
                back = known(i, j - 1)
                first = isinstance(i, int) and num(i, j) == 0
                if cur:
                    scores(i, j, 0)
                    scores(i, j, 1)
                    if first:
                        pe.wait_ge(s_g2, 5)
                    state_waits(i, j, 0)
                    gate(i, j)
                if known(i, j - 2):
                    if isinstance(i, int) and num(i, j) == 2:
                        pe.wait_ge(s_woready, 4)
                if cur:
                    state_step(i, j, 0)
                if known(i, j - 2):
                    project_o(i, j - 2)
                if nxt:
                    project_kv(i, j + 1)
                if cur:
                    scores(i, j, 2)
                if first:
                    transpose_xq(0, 0)
                if nxt:
                    project_qg(i, j + 1)
                if first:
                    pe.wait_ge(s_w2q, 6)
                    ffn(0, 0)
                if cur:
                    state_waits(i, j, 1)
                    scores(i, j, 3)
                    state_step(i, j, 1)
                if nxt:
                    transpose_xq(i, j + 1)
                if norm:
                    transpose_x(i, j + 2)
                if nxt:
                    transpose_qk(i, j + 1)
                if cur and not nxt:
                    from_state(i, j)
                if cur:
                    from_chunk(i, j)
                if nxt:
                    ffn(i, j + 1)
                    from_state(i, j)
                if cur and not nxt:
                    add_chunk(i, j)
                if back and not cur:
                    keep_warm(6)
                if back:
                    transpose_o(i, j - 1)
                if nxt:
                    add_chunk(i, j)
                if nxt:
                    transpose_g1(i, j + 1)

            steps(step, prologue)(pe)


_INS = ['L0_attn_x', 'L0_attn_log_decay', 'L0_attn_Wq', 'L0_attn_Wk', 'L0_attn_Wv', 'L0_attn_Wo', 'L0_attn_Wg1',
        'L0_attn_Wg2', 'L0_attn_norm_w', 'L0_ffn_input2', 'L0_ffn_scale', 'L0_ffn_scale1']
_OUTS = [((4, 512, 256), 'float32')]


def kernel(**inputs):
    import numpy as _np
    import concourse.bacc as _bacc
    from concourse import mybir as _mybir
    from concourse.bass_utils import run_bass_kernel_spmd as _run

    nc = _bacc.Bacc("TRN2", target_bir_lowering=False, num_devices=1)
    arrays, args = {}, []
    for name in _INS:
        a = _np.ascontiguousarray(inputs[name])
        if a.ndim == 0:
            a = a.reshape(1)
        arrays[f"in_{name}_dram"] = a
        args.append(nc.dram_tensor(f"in_{name}_dram", a.shape, _mybir.dt.from_np(a.dtype), kind="ExternalInput").ap())
    for i, (shape, dtype) in enumerate(_OUTS):
        dt = _mybir.dt.from_np(_np.dtype(dtype))
        args.append(nc.dram_tensor(f"out_{i}_dram", shape, dt, kind="ExternalOutput").ap())
    layer_kernel(nc, *args)
    r = _run(nc, [arrays], core_ids=[0])
    return r.results[0]["out_0_dram"]
```
